# Optimizing a Trainium2 kernel written in Bass

```python
import numpy as np
import jax
import jax.numpy as jnp

def _softmax(x, axis=-1):
    return jax.nn.softmax(x, axis=axis)

def _gelu(x):
    return jax.nn.gelu(x, approximate=True)

def _silu(x):
    return jax.nn.silu(x)

def _sigmoid(x):
    return jax.nn.sigmoid(x)

def _layernorm(x, axis=-1, eps=1e-05):
    m = jnp.mean(x, axis=axis, keepdims=True)
    v = jnp.var(x, axis=axis, keepdims=True)
    return (x - m) / jnp.sqrt(v + eps)

def _scatter_add(tgt, idx, src, axis=0):
    return tgt.at[idx].add(src)

def _segment_sum(src, seg, n):
    return jax.ops.segment_sum(src, seg, n)
kernel_name = 'mk_adj_resnorm_d1_adj_r2_7dce71'

def setup_inputs(seed: int=0):
    np.random.seed(seed)
    _w = jnp.asarray

    def _rec_inputs():
        import jax
        import jax.numpy as jnp
        _gk = jax.random.key(seed)
        x = -0.0005207 + 1.001 * jax.random.normal(jax.random.fold_in(_gk, 1), (1354, 256), jnp.float32)
        _a = jax.random.bernoulli(jax.random.fold_in(_gk, 2), 0.0118168, (1354, 1354))
        adj = _a.astype(jnp.int32)
        return (x, adj)
    x, adj = _rec_inputs()

    def _L0_gnn_setup():
        import jax, jax.numpy as jnp
        import numpy as np
        N = 2048
        STATE_DIM = 256
        OUTPUT_DIM = 256
        N_STEPS = 5
        W_STD = 0.02

        def _lin_params(key, out_dim, in_dim):
            W = jax.random.normal(key, (out_dim, in_dim), dtype=jnp.float32) * W_STD
            b = jnp.zeros((out_dim,), dtype=jnp.float32)
            return (W, b)
        key = jax.random.key(seed)
        ks = jax.random.split(key, 10)
        prop_state = jax.random.normal(ks[0], (N, STATE_DIM), dtype=jnp.float32)
        A = jax.random.randint(ks[1], (N, N), 0, 2, dtype=jnp.int64)
        in_W, in_b = _lin_params(ks[2], STATE_DIM, STATE_DIM)
        out_W, out_b = _lin_params(ks[3], STATE_DIM, STATE_DIM)
        r_W, r_b = _lin_params(ks[4], STATE_DIM, 3 * STATE_DIM)
        z_W, z_b = _lin_params(ks[5], STATE_DIM, 3 * STATE_DIM)
        h_W, h_b = _lin_params(ks[6], STATE_DIM, 3 * STATE_DIM)
        o1_W, o1_b = _lin_params(ks[7], STATE_DIM, STATE_DIM)
        o2_W, o2_b = _lin_params(ks[8], OUTPUT_DIM, STATE_DIM)
        return {'prop_state': prop_state, 'A': A, 'in_W': in_W, 'in_b': in_b, 'out_W': out_W, 'out_b': out_b, 'r_W': r_W, 'r_b': r_b, 'z_W': z_W, 'z_b': z_b, 'h_W': h_W, 'h_b': h_b, 'o1_W': o1_W, 'o1_b': o1_b, 'o2_W': o2_W, 'o2_b': o2_b}
    _L0_gnn_all = _L0_gnn_setup()
    _L0_gnn_in = {k: v for k, v in _L0_gnn_all.items() if k in ('in_W', 'in_b', 'out_W', 'out_b', 'r_W', 'r_b', 'z_W', 'z_b', 'h_W', 'h_b', 'o1_W', 'o1_b', 'o2_W', 'o2_b')}
    del _L0_gnn_all
    return {'x': x, 'adj': adj, 'L0_gnn_in_W': _L0_gnn_in['in_W'], 'L0_gnn_in_b': _L0_gnn_in['in_b'], 'L0_gnn_out_W': _L0_gnn_in['out_W'], 'L0_gnn_out_b': _L0_gnn_in['out_b'], 'L0_gnn_r_W': _L0_gnn_in['r_W'], 'L0_gnn_r_b': _L0_gnn_in['r_b'], 'L0_gnn_z_W': _L0_gnn_in['z_W'], 'L0_gnn_z_b': _L0_gnn_in['z_b'], 'L0_gnn_h_W': _L0_gnn_in['h_W'], 'L0_gnn_h_b': _L0_gnn_in['h_b'], 'L0_gnn_o1_W': _L0_gnn_in['o1_W'], 'L0_gnn_o1_b': _L0_gnn_in['o1_b'], 'L0_gnn_o2_W': _L0_gnn_in['o2_W'], 'L0_gnn_o2_b': _L0_gnn_in['o2_b']}

def reference(x, adj, L0_gnn_in_W, L0_gnn_in_b, L0_gnn_out_W, L0_gnn_out_b, L0_gnn_r_W, L0_gnn_r_b, L0_gnn_z_W, L0_gnn_z_b, L0_gnn_h_W, L0_gnn_h_b, L0_gnn_o1_W, L0_gnn_o1_b, L0_gnn_o2_W, L0_gnn_o2_b):
    import jax
    import jax.numpy as jnp

    def _L0_gnn_ref(prop_state, A, in_W, in_b, out_W, out_b, r_W, r_b, z_W, z_b, h_W, h_b, o1_W, o1_b, o2_W, o2_b):
        import jax, jax.numpy as jnp
        import numpy as np
        N = 2048
        STATE_DIM = 256
        OUTPUT_DIM = 256
        N_STEPS = 5
        W_STD = 0.02

        def _lin_params(key, out_dim, in_dim):
            W = jax.random.normal(key, (out_dim, in_dim), dtype=jnp.float32) * W_STD
            b = jnp.zeros((out_dim,), dtype=jnp.float32)
            return (W, b)
        Af = A.astype(prop_state.dtype)
        AfT = Af.T
        state = prop_state
        for _ in range(N_STEPS):
            s_in = state @ in_W.T + in_b
            s_out = state @ out_W.T + out_b
            a_in = Af @ s_in
            a_out = AfT @ s_out
            a = jnp.concatenate([a_in, a_out, state], axis=-1)
            r = jax.nn.sigmoid(a @ r_W.T + r_b)
            z = jax.nn.sigmoid(a @ z_W.T + z_b)
            joined = jnp.concatenate([a_in, a_out, r * state], axis=-1)
            h_hat = jnp.tanh(joined @ h_W.T + h_b)
            state = (1.0 - z) * state + z * h_hat
        out = jnp.tanh(state @ o1_W.T + o1_b) @ o2_W.T + o2_b
        return out
    x = _layernorm(x + _L0_gnn_ref(x, adj, L0_gnn_in_W, L0_gnn_in_b, L0_gnn_out_W, L0_gnn_out_b, L0_gnn_r_W, L0_gnn_r_b, L0_gnn_z_W, L0_gnn_z_b, L0_gnn_h_W, L0_gnn_h_b, L0_gnn_o1_W, L0_gnn_o1_b, L0_gnn_o2_W, L0_gnn_o2_b), axis=-1)
    return x

_drawn_inputs = setup_inputs


def setup_inputs(seed=0):
    import zlib

    import numpy as np

    out = dict(_drawn_inputs(seed))
    spreads = {'L0_gnn_in_b': (0.0, 0.1),
     'L0_gnn_out_b': (0.0, 0.1),
     'L0_gnn_r_b': (0.0, 0.8),
     'L0_gnn_z_b': (0.0, 0.8),
     'L0_gnn_h_b': (0.0, 0.8),
     'L0_gnn_o1_b': (0.0, 0.1),
     'L0_gnn_o2_b': (0.0, 0.1)}
    factors = {'L0_gnn_r_W': 8.0}
    for name, (base, spread) in spreads.items():
        noise = np.random.default_rng([zlib.crc32(name.encode()), seed]).standard_normal(out[name].shape)
        drawn = base * np.exp(spread * noise) if base else spread * noise
        out[name] = jnp.asarray(drawn.astype(out[name].dtype))
    for name, factor in factors.items():
        out[name] = (out[name] * factor).astype(out[name].dtype)
    return out
```

```python
import numpy as np
import concourse.bass as bass
from concourse import mybir

F32 = mybir.dt.float32
F32R = mybir.dt.float32r
I32 = mybir.dt.int32
ALU = mybir.AluOpType
ACT = mybir.ActivationFunctionType

P = 128
BANK = 512
STEPS = 5
EPS = 1e-5


def gated_graph_network(nc, x, adj, in_W, in_b, out_W, out_b, r_W, r_b, z_W, z_b, h_W, h_b,
                        o1_W, o1_b, o2_W, o2_b, out):
    N, D = x.shape
    HALVES = D // P
    TILES = -(-N // P)
    ROWS = [min(P, N - j * P) for j in range(TILES)]
    CHUNKS = [(c, min(BANK, N - c)) for c in range(0, N, BANK)]
    NC = len(CHUNKS)
    TPC = BANK // P
    GATES = 3 * HALVES
    GW = 3 * D
    KT = 3 * HALVES
    FULL, LAST = TILES - 1, ROWS[-1]
    assert D == 2 * P and NC == 3 and TILES == 11 and FULL == 10

    STREAMED = [5, 6, 7, 8, 9]
    RESIDENT = [j for j in range(TILES) if j not in STREAMED]
    NS, NR = len(STREAMED), len(RESIDENT)

    base = -(-nc.sbuf_base // 32) * 32

    def place(name, shape, dt, at):
        size = int(np.prod(shape[1:])) * 4
        return nc.alloc_sbuf_tensor_at(name, shape, dt, offset=base + at), at + -(-size // 32) * 32

    at = 0
    an_at = at
    an_res, at = place("an_res", [P, NR, N], F32R, at)
    atr_at = at
    at_res, at = place("at_res", [P, NR, N], F32R, at)
    s_hi, at = place("s_hi", [P, TILES, D], F32R, at)
    s_lo, at = place("s_lo", [P, TILES, D], F32R, at)
    w_hi, at = place("w_hi", [P, KT, GW], F32R, at)
    w_lo, at = place("w_lo", [P, KT, GW], F32R, at)
    deg, at = place("deg", [P, N], F32R, at)
    degw, at = place("degw", [P, GW], F32R, at)
    st, at = place("st", [P, HALVES, N], F32, at)
    ring_at = at
    ring_n, at = place("ring_n", [P, NS, BANK], F32R, at)
    ring_t, at = place("ring_t", [P, NS, BANK], F32R, at)
    ident, at = place("ident", [P, P], F32, at)
    bias, at = place("bias", [P, GATES + HALVES], F32, at)
    io_b, at = place("io_b", [P, 2 * HALVES], F32, at)
    masks, at = place("masks", [P, 2], F32, at)
    work_at = at
    a_hi, at = place("a_hi", [P, 4, BANK], F32R, at)
    a_lo, at = place("a_lo", [P, 4, BANK], F32R, at)
    r_buf, at = place("r_buf", [P, HALVES, BANK], F32, at)
    z_buf, at = place("z_buf", [P, HALVES, BANK], F32, at)
    h_buf, at = place("h_buf", [P, HALVES, BANK], F32, at)
    rs_hi, at = place("rs_hi", [P, HALVES, BANK], F32R, at)
    rs_lo, at = place("rs_lo", [P, HALVES, BANK], F32R, at)
    sc_at = at
    sc_hi, at = place("sc_hi", [P, HALVES, BANK], F32R, at)
    sc_lo, at = place("sc_lo", [P, HALVES, BANK], F32R, at)

    w_nat, q = place("w_nat", [P, 3, HALVES, GW], F32, atr_at)
    x_nat, q = place("x_nat", [P, TILES, D], F32, q)
    assert q <= atr_at + 4 * NR * N
    wt_f, q = place("wt_f", [P, 2 * HALVES, GW], F32, ring_at)
    io_nat, q = place("io_nat", [P, 2, HALVES, D], F32, q)
    b_sel, q = place("b_sel", [P, 2 * HALVES, P], F32, q)
    assert q <= ring_at + 8 * NS * BANK
    NI = 3
    a_int, q = place("a_int", [P, NI, N], I32, work_at)
    an_stage, q = place("an_stage", [P, 2, N], F32R, q)
    at_stage, q = place("at_stage", [P, 2, NS, P], F32R, q)
    e_sel, q = place("e_sel", [P, 2, P], F32R, q)
    c_lo, q = place("c_lo", [P, GW], F32, q)
    assert q <= sc_at
    x_end, q = place("x_end", [P, TILES, D], F32, an_at)
    o_nat, q = place("o_nat", [P, 2, HALVES, D], F32, q)
    o_bias, q = place("o_bias", [P, D], F32, q)
    o_hi, q = place("o_hi", [P, 2, HALVES, D], F32R, q)
    o_lo, q = place("o_lo", [P, 2, HALVES, D], F32R, q)
    stats, q = place("stats", [P, TILES, 6], F32, q)
    mean_var, q = place("mean_var", [P, TILES, 2], F32, q)
    std, q = place("std", [P, TILES], F32, q)
    rstd, q = place("rstd", [P, TILES], F32, q)
    eps_col, q = place("eps_col", [P, 1], F32, q)
    assert q <= ring_at

    ps = nc.alloc_psum_tensor("ps", [P, 8, BANK], F32)
    ACC, GB, TB = 0, 4, 7

    far_n = nc.dram_tensor("far_n", [NS, P, N], F32, kind="Internal").ap()
    far_t = nc.dram_tensor("far_t", [NS, P, N], F32, kind="Internal").ap()

    S = nc.alloc_semaphore
    weights_in = S("weights_in")
    x_in = S("x_in")
    small_in = S("small_in")
    adj_in = [S(f"adj_in{b}") for b in range(NI)]
    consts = S("consts")
    selected = S("selected")
    esel_zero = S("esel_zero")
    c_steps = S("c_steps")
    prep_ready = S("prep_ready")
    prep_hi = S("prep_hi")
    prep_out = S("prep_out")
    converted = S("converted")
    at_ready = S("at_ready")
    at_act = S("at_act")
    at_dve = S("at_dve")
    at_used = S("at_used")
    far_n_out = [S(f"far_n_out{b}") for b in range(2)]
    far_t_out = [S(f"far_t_out{b}") for b in range(2)]
    deg_ready = S("deg_ready")
    streamed_in = [S(f"streamed_in{k}") for k in range(NS)]
    streamed_used = [S(f"streamed_used{k}") for k in range(NS)]
    acc_ready = S("acc_ready")
    a_hi_ready = S("a_hi_ready")
    a_lo_ready = S("a_lo_ready")
    gate_ready = S("gate_ready")
    gate_act = S("gate_act")
    rs_ready = S("rs_ready")
    rs_hi_ready = S("rs_hi_ready")
    rs_lo_ready = S("rs_lo_ready")
    diff_ready = S("diff_ready")
    zdiff_ready = S("zdiff_ready")
    state_ready = S("state_ready")
    sc_hi_ready = S("sc_hi_ready")
    sc_lo_ready = S("sc_lo_ready")
    turned = S("turned")
    s_hi_ready = S("s_hi_ready")
    s_lo_ready = S("s_lo_ready")
    end_in = S("end_in")
    o_ready = S("o_ready")
    o_hi_ready = S("o_hi_ready")
    o_lo_ready = S("o_lo_ready")
    t_sum = S("t_sum")
    t_act = S("t_act")
    t_hi_ready = S("t_hi_ready")
    t_lo_ready = S("t_lo_ready")
    y_sum = S("y_sum")
    x_bias = S("x_bias")
    eps_ready = S("eps_ready")
    y_ready = S("y_ready")
    st_ready = S("st_ready")
    mv_ready = S("mv_ready")
    std_ready = S("std_ready")
    rstd_ready = S("rstd_ready")
    normed = S("normed")
    stored = S("stored")

    def tiles_of(c):
        return range(c * TPC, min((c + 1) * TPC, TILES))

    TURNS = [(8, 9), (10,), (0, 1), (2, 3), (4, 5), (6, 7)]
    NT = len(TURNS)
    NAT0, ST0 = 2, HALVES * NC

    PREP = ([("wt", k) for k in range(2 * HALVES)] + [("ws", k) for k in range(HALVES)]
            + [("fold", k) for k in range(2 * HALVES)] + [("bias", 0)]
            + [("xt", k) for k in range(HALVES * NC)])
    GH = GW // 2

    def prep_area(n):
        return ps[:, 2 * (n % 4):2 * (n % 4) + 2, 0:GH]

    def prep_done_counts(n):
        xt = sum(1 for k, _ in PREP[:n + 1] if k == "xt")
        return n + 1 - xt, xt

    AT_BANKS = 5

    def at_bank(m):
        return 3 + m % AT_BANKS

    AT_GROUPS = [RESIDENT[0:4], [RESIDENT[4], RESIDENT[5], STREAMED[4]], STREAMED[0:4]]

    def at_copier(m):
        i, g = divmod(m, 3)
        return (0, i % 2, 1)[g]

    def at_counts(m):
        who = [at_copier(k) for k in range(m + 1)]
        return who.count(0), who.count(1)

    def an_tile(i):
        return an_res[:, RESIDENT.index(i), :] if i in RESIDENT else an_stage[:, STREAMED.index(i) % 2, :]

    def end_state(c, kt):
        cw = CHUNKS[c][1]
        if c % 2 == 0:
            return sc_hi[:, kt, 0:cw], sc_lo[:, kt, 0:cw]
        return a_hi[:, 2 + kt, 0:cw], a_lo[:, 2 + kt, 0:cw]

    def end_hidden(c, kt):
        cw = CHUNKS[c][1]
        if c % 2 == 0:
            return rs_hi[:, kt, 0:cw], rs_lo[:, kt, 0:cw]
        return a_hi[:, kt, 0:cw], a_lo[:, kt, 0:cw]

    def state_cols(half, c):
        c0, cw = CHUNKS[c]
        return st[:, half, c0:c0 + cw]

    def copy_at(eng, copy, who, done):
        for m in range(3 * TILES):
            if at_copier(m) != who:
                continue
            i, g = divmod(m, 3)
            r, b = ROWS[i], at_bank(m)
            eng.wait_ge(at_ready, m + 1)
            if g > 0 and i >= 2:
                eng.wait_ge(far_t_out[i % 2], 16 * (i // 2))
                eng.wait_ge(at_used, i - 1)
            src = ps[:, b, 0:4 * P].rearrange("p (k n) -> p k n", k=4)[:, :, 0:r]
            if g == 0:
                copy(at_res[:, 0:4, i * P:i * P + r], src).then_inc(done, 1)
            elif g == 1:
                copy(at_res[:, 4, i * P:i * P + r], ps[:, b, 0:r])
                copy(at_res[0:LAST, 5, i * P:i * P + r], ps[0:LAST, b, P:P + r])
                copy(at_stage[:, i % 2, 4, 0:r], ps[:, b, 2 * P:2 * P + r]).then_inc(done, 1)
            else:
                copy(at_stage[:, i % 2, 0:4, 0:r], src).then_inc(done, 1)

    block = nc.Block()
    block.__enter__()

    @block.sync
    def _(sp):
        for g, w in enumerate((r_W, z_W, h_W)):
            sp.dma_start(w_nat[:, g], w.rearrange("(m p) k -> p m k", p=P)).then_inc(weights_in, 16)
        for g, w in enumerate((in_W, out_W)):
            sp.dma_start(io_nat[:, g], w.rearrange("(m p) k -> p m k", p=P)).then_inc(weights_in, 16)
        def store_blocks(i):
            n_act, n_dve = at_counts(3 * i + 2)
            sp.wait_ge(at_act, n_act)
            sp.wait_ge(at_dve, n_dve)
            sp.dma_start(far_t[:, :, i * P:i * P + ROWS[i]].rearrange("k p n -> p k n"),
                         at_stage[:, i % 2, :, 0:ROWS[i]].bitcast(F32)).then_inc(far_t_out[i % 2], 16)

        for i in range(TILES):
            if i >= NI:
                sp.wait_ge(converted, i - NI + 1)
            sp.dma_start(a_int[0:ROWS[i], i % NI], adj[i * P:i * P + ROWS[i], :]).then_inc(adj_in[i % NI], 16)
            if i >= 1 and i - 1 in STREAMED:
                k = STREAMED.index(i - 1)
                sp.wait_ge(converted, i)
                sp.dma_start(far_n[k], an_stage[:, k % 2, :].bitcast(F32)).then_inc(far_n_out[k % 2], 16)
            if i >= NI + 1:
                store_blocks(i - NI - 1)
        for i in range(TILES - NI - 1, TILES):
            store_blocks(i)
        sp.wait_ge(far_n_out[0], 16 * ((NS + 1) // 2))
        sp.wait_ge(far_n_out[1], 16 * (NS // 2))
        sp.wait_ge(far_t_out[0], 16 * ((TILES + 1) // 2))
        sp.wait_ge(far_t_out[1], 16 * (TILES // 2))

        def stream(c, used):
            c0, cw = CHUNKS[c]
            for k in range(NS):
                if used is not None:
                    sp.wait_ge(streamed_used[k], used)
                sp.dma_start(ring_n[:, k, 0:cw].bitcast(F32), far_n[k, :, c0:c0 + cw]).then_inc(streamed_in[k], 16)
                sp.dma_start(ring_t[:, k, 0:cw].bitcast(F32), far_t[k, :, c0:c0 + cw]).then_inc(streamed_in[k], 16)

        stream(0, None)
        with sp.Fori(0, STEPS - 1) as i:
            for c in range(NC):
                stream((c + 1) % NC, i * NC + c + 1)
        for c in range(NC - 1):
            stream(c + 1, (STEPS - 1) * NC + c + 1)
        sp.wait_ge(acc_ready, 4 * NC * STEPS)
        for g, w in enumerate((o1_W, o2_W)):
            sp.dma_start(o_nat[:, g], w.rearrange("(m p) k -> p m k", p=P)).then_inc(end_in, 16)
        sp.dma_start(o_bias[:, :], o2_b.rearrange("(a d) -> a d", a=1).to_broadcast([P, D])).then_inc(end_in, 16)
        sp.dma_start(x_end[:, 0:FULL], x[0:FULL * P, :].rearrange("(t p) d -> p t d", p=P)).then_inc(end_in, 16)
        sp.dma_start(x_end[0:LAST, FULL], x[FULL * P:N, :]).then_inc(end_in, 16)
        for c in range(NC):
            ts = tiles_of(c)
            sp.wait_ge(normed, ts[-1] + 1)
            full = [t for t in ts if t < FULL]
            sp.dma_start(out[full[0] * P:(full[-1] + 1) * P, :].rearrange("(t p) d -> p t d", p=P),
                         x_end[:, full[0]:full[-1] + 1]).then_inc(stored, 16)
        sp.dma_start(out[FULL * P:N, :], x_end[0:LAST, FULL]).then_inc(stored, 16)
        sp.wait_ge(stored, 16 * (NC + 1))

    @block.gpsimd
    def _(pool):
        nc.gpsimd.memset(ident[:], 0.0).then_inc(consts, 1)
        pool.wait_ge(consts, 1)
        nc.gpsimd.affine_select(out=ident[:], in_=ident[:], compare_op=ALU.not_equal, fill=1.0, base=0,
                                pattern=[[-1, P]], channel_multiplier=1).then_inc(consts, 1)
        for i in range(TILES):
            rows = ROWS[i]
            pool.wait_ge(adj_in[i % NI], 16 * (i // NI + 1))
            if i in STREAMED and STREAMED.index(i) >= 2:
                k = STREAMED.index(i)
                pool.wait_ge(at_ready, 3 * (i - 1))
                pool.wait_ge(far_n_out[k % 2], 16 * (k // 2))
            nc.gpsimd.tensor_copy(an_tile(i)[0:rows], a_int[0:rows, i % NI]).then_inc(converted, 1)

    @block.tensor
    def _(pe):
        def three(dst, kt, cols, hi, lo, start, stop, wh=w_hi, wl=w_lo):
            nc.tensor.matmul(dst, wh[:, kt, cols], hi, start=start, stop=False)
            nc.tensor.matmul(dst, wh[:, kt, cols], lo, start=False, stop=False)
            return nc.tensor.matmul(dst, wl[:, kt, cols], hi, start=False, stop=stop)

        pe.wait_ge(consts, 2)
        pe.wait_ge(weights_in, 16 * 5)
        for n, (kind, k) in enumerate(PREP):
            if n >= 4:
                n_out, n_state = prep_done_counts(n - 4)
                pe.wait_ge(prep_out, n_out)
                if n_state:
                    pe.wait_ge(state_ready, n_state)
            area = prep_area(n)
            if kind in ("wt", "ws"):
                qt = k if kind == "wt" else 2 * HALVES + k
                for o in range(GATES):
                    g, m = divmod(o, HALVES)
                    dst = area[:, o // 3, (o % 3) * P:(o % 3 + 1) * P]
                    last = nc.tensor.transpose(dst, w_nat[:, g, m, qt * P:(qt + 1) * P], ident[:])
            elif kind == "fold":
                which, kt = divmod(k, HALVES)
                if k == 0:
                    pe.wait_ge(prep_out, 2 * HALVES)
                for b in range(2):
                    for qh in range(HALVES):
                        last = nc.tensor.matmul(area[:, b], io_nat[:, which, qh, kt * P:(kt + 1) * P],
                                                wt_f[:, which * HALVES + qh, b * GH:(b + 1) * GH],
                                                start=(qh == 0), stop=(qh == HALVES - 1))
            elif kind == "bias":
                pe.wait_ge(selected, 2)
                for b in range(2):
                    for qt in range(2 * HALVES):
                        last = nc.tensor.matmul(area[:, b], b_sel[:, qt], wt_f[:, qt, b * GH:(b + 1) * GH],
                                                start=(qt == 0), stop=(qt == 2 * HALVES - 1))
            else:
                half, c = divmod(k, NC)
                if k == 0:
                    pe.wait_ge(x_in, 32)
                for j in tiles_of(c):
                    r = ROWS[j]
                    last = nc.tensor.transpose(ps[:, 2 * (n % 4), (j % TPC) * P:(j % TPC) * P + r],
                                               x_nat[0:r, j, half * P:(half + 1) * P], ident[0:r, 0:r])
            last.then_inc(prep_ready, 1)
        n_out, n_state = prep_done_counts(len(PREP) - 1)
        pe.wait_ge(prep_out, n_out)
        pe.wait_ge(state_ready, n_state)

        def sum_blocks(i):
            n_act, n_dve = at_counts(3 * i + 2)
            pe.wait_ge(at_act, n_act)
            pe.wait_ge(at_dve, n_dve)
            c, off = divmod(i, TPC)
            dst = ps[:, c, off * P:off * P + ROWS[i]]
            for j in range(TILES):
                src = (at_res[0:ROWS[j], RESIDENT.index(j), i * P:i * P + ROWS[i]] if j in RESIDENT
                       else at_stage[0:ROWS[j], i % 2, STREAMED.index(j), 0:ROWS[i]])
                last = nc.tensor.matmul(dst, e_sel[0:ROWS[j], 0], src, start=False,
                                        stop=(i == TILES - 1 and j == TILES - 1), skip_group_check=True)
            last.then_inc(at_used, 1)

        pe.wait_ge(selected, 4)
        for i in range(TILES):
            pe.wait_ge(converted, i + 1)
            tile = an_tile(i)
            for c, (c0, cw) in enumerate(CHUNKS):
                nc.tensor.matmul(ps[:, c, 0:cw], e_sel[0:ROWS[i], 1], tile[0:ROWS[i], c0:c0 + cw],
                                 start=(i == 0), stop=False, skip_group_check=True)
            for g, group in enumerate(AT_GROUPS):
                m = 3 * i + g
                if m >= AT_BANKS:
                    n_act, n_dve = at_counts(m - AT_BANKS)
                    pe.wait_ge(at_act, n_act)
                    if n_dve:
                        pe.wait_ge(at_dve, n_dve)
                for k, j in enumerate(group):
                    last = nc.tensor.transpose(ps[0:ROWS[j], at_bank(m), k * P:k * P + ROWS[i]],
                                               tile[0:ROWS[i], j * P:j * P + ROWS[j]].bitcast(F32),
                                               ident[0:ROWS[i], 0:ROWS[i]])
                last.then_inc(at_ready, 1)
            if i >= 1:
                sum_blocks(i - 1)
        sum_blocks(TILES - 1)
        pe.wait_ge(a_lo_ready, NC)

        def turn(i, t):
            pe.wait_ge(s_lo_ready, NAT0 + i * NT + t)
            for n, j in enumerate(TURNS[t]):
                for half in range(HALVES):
                    last = nc.tensor.transpose(ps[0:ROWS[j], TB, n * D + half * P:n * D + (half + 1) * P],
                                               st[:, half, j * P:j * P + ROWS[j]], ident[:])
            last.then_inc(turned, 1)

        def aggregate(i, c):
            c0, cw = CHUNKS[c]
            pe.wait_ge(a_lo_ready, NC + i * 4 * NC + 4 * c)
            if c == 0:
                pe.wait_ge(s_hi_ready, NAT0 + i * NT)
                pe.wait_ge(s_lo_ready, NAT0 + i * NT)
            for j in range(TILES):
                r = ROWS[j]
                if c == 0 and j == 6:
                    pe.wait_ge(state_ready, ST0 + i * NC * HALVES)
                    turn(i, 0)
                if c == 0 and j == 7:
                    turn(i, 1)
                if c == 0 and j == TURNS[0][0]:
                    pe.wait_ge(s_hi_ready, NAT0 + i * NT + 1)
                    pe.wait_ge(s_lo_ready, NAT0 + i * NT + 1)
                if c == 0 and j == TURNS[1][0]:
                    pe.wait_ge(s_hi_ready, NAT0 + i * NT + 2)
                    pe.wait_ge(s_lo_ready, NAT0 + i * NT + 2)
                if j in STREAMED:
                    k = STREAMED.index(j)
                    pe.wait_ge(streamed_in[k], i * 32 * NC + 32 * (c + 1))
                    rows_t, rows_n = ring_t[0:r, k, 0:cw], ring_n[0:r, k, 0:cw]
                else:
                    k = RESIDENT.index(j)
                    rows_t, rows_n = at_res[0:r, k, c0:c0 + cw], an_res[0:r, k, c0:c0 + cw]
                for q in range(4):
                    rows, half = (rows_t, rows_n)[q // HALVES], q % HALVES
                    dst = ps[:, ACC + q, 0:cw]
                    nc.tensor.matmul(dst, s_hi[0:r, j, half * P:(half + 1) * P], rows, start=(j == 0), stop=False)
                    last = nc.tensor.matmul(dst, s_lo[0:r, j, half * P:(half + 1) * P], rows, start=False,
                                            stop=(j == TILES - 1))
                    if j == TILES - 1:
                        last.then_inc(acc_ready, 1)
                if j in STREAMED:
                    last.then_inc(streamed_used[STREAMED.index(j)], 1)

        def gates(i, c):
            c0, cw = CHUNKS[c]
            g0 = i * GATES * NC + GATES * c
            base4 = i * 4 * NC + 4 * c
            base2 = i * HALVES * NC + HALVES * c

            def dst(o):
                return ps[:, GB + o % 3, 0:cw]

            def state_part(o):
                for half in range(HALVES):
                    three(dst(o), 2 * HALVES + half, slice(o * P, (o + 1) * P),
                          sc_hi[:, half, 0:cw], sc_lo[:, half, 0:cw], half == 0, False)

            def degree_part(o, start):
                nc.tensor.matmul(dst(o), degw[:, o * P:(o + 1) * P], deg[:, c0:c0 + cw], start=start, stop=False)

            def sums_part(o, stop):
                for q in range(4):
                    if o == 0:
                        pe.wait_ge(a_hi_ready, base4 + q + 1)
                        pe.wait_ge(a_lo_ready, NC + base4 + q + 1)
                    last = three(dst(o), q, slice(o * P, (o + 1) * P), a_hi[:, q, 0:cw], a_lo[:, q, 0:cw],
                                 False, stop and q == 3)
                return last

            if c > 0:
                pe.wait_ge(gate_act, g0)
            pe.wait_ge(sc_hi_ready, base2 + HALVES)
            pe.wait_ge(sc_lo_ready, base2 + HALVES)
            for o in range(3):
                state_part(o)
                degree_part(o, False)
            for o in range(4):
                if o == 3:
                    pe.wait_ge(gate_act, g0 + 1)
                    state_part(o)
                    degree_part(o, False)
                sums_part(o, True).then_inc(gate_ready, 1)
                if c == NC - 1:
                    turn(i, 2 + o)
            for o in range(4, GATES):
                pe.wait_ge(gate_act, g0 + o - 2)
                degree_part(o, True)
                sums_part(o, False)
                for half in range(HALVES):
                    if o == 4:
                        pe.wait_ge(rs_hi_ready, base2 + half + 1)
                        pe.wait_ge(rs_lo_ready, base2 + half + 1)
                    last = three(dst(o), 2 * HALVES + half, slice(o * P, (o + 1) * P),
                                 rs_hi[:, half, 0:cw], rs_lo[:, half, 0:cw], False, half == HALVES - 1)
                last.then_inc(gate_ready, 1)

        with pe.Fori(0, STEPS) as i:
            for c in range(NC):
                aggregate(i, c)
                gates(i, c)

        pe.wait_ge(a_lo_ready, NC + 4 * NC * STEPS)
        pe.wait_ge(end_in, 16 * 5)
        for g in range(2):
            for kt in range(HALVES):
                for m in range(HALVES):
                    last = nc.tensor.transpose(ps[:, g, kt * D + m * P:kt * D + (m + 1) * P],
                                               o_nat[:, g, m, kt * P:(kt + 1) * P], ident[:])
            last.then_inc(o_ready, 1)

        def hidden(c):
            cw = CHUNKS[c][1]
            n_sc = HALVES * (NC * STEPS + c + 1)
            pe.wait_ge(sc_hi_ready, n_sc)
            pe.wait_ge(sc_lo_ready, n_sc)
            for m in range(HALVES):
                n = HALVES * c + m
                if n >= 3:
                    pe.wait_ge(t_act, n - 2)
                dst = ps[:, GB + n % 3, 0:cw]
                for kt in range(HALVES):
                    hi, lo = end_state(c, kt)
                    last = three(dst, 0, slice(m * P, (m + 1) * P), hi, lo, kt == 0, kt == HALVES - 1,
                                 o_hi[:, 0, kt:kt + 1], o_lo[:, 0, kt:kt + 1])
                last.then_inc(t_sum, 1)

        def head(c):
            pe.wait_ge(t_hi_ready, HALVES * (c + 1))
            pe.wait_ge(t_lo_ready, HALVES * (c + 1))
            for j in tiles_of(c):
                r = ROWS[j]
                if j >= 4:
                    pe.wait_ge(y_ready, j - 3)
                dst = ps[0:r, ACC + j % 4, 0:D]
                off = (j % TPC) * P
                for kt in range(HALVES):
                    hi, lo = end_hidden(c, kt)
                    hi, lo = hi[:, off:off + r], lo[:, off:off + r]
                    nc.tensor.matmul(dst, hi, o_hi[:, 1, kt], start=(kt == 0), stop=False)
                    nc.tensor.matmul(dst, hi, o_lo[:, 1, kt], start=False, stop=False)
                    last = nc.tensor.matmul(dst, lo, o_hi[:, 1, kt], start=False, stop=(kt == HALVES - 1))
                last.then_inc(y_sum, 1)

        pe.wait_ge(gate_act, GATES * NC * STEPS)
        pe.wait_ge(o_hi_ready, 2)
        pe.wait_ge(o_lo_ready, 2)
        hidden(0)
        hidden(1)
        head(0)
        hidden(2)
        head(1)
        head(2)

    @block.scalar
    def _(act):
        act.dma_start(x_nat[:, 0:FULL], x[0:FULL * P, :].rearrange("(t p) d -> p t d", p=P)).then_inc(x_in, 16)
        act.dma_start(x_nat[0:LAST, FULL], x[FULL * P:N, :]).then_inc(x_in, 16)
        for n, b in enumerate((r_b, z_b, h_b, o1_b)):
            act.dma_start(bias[:, n * HALVES:(n + 1) * HALVES],
                          b.rearrange("(m p) -> p m", p=P),
                          allow_slow_non_contiguous=True).then_inc(small_in, 16)
        for n, b in enumerate((in_b, out_b)):
            act.dma_start(io_b[:, n * HALVES:(n + 1) * HALVES],
                          b.rearrange("(m p) -> p m", p=P),
                          allow_slow_non_contiguous=True).then_inc(small_in, 16)
        for n, (kind, k) in enumerate(PREP):
            if kind == "wt":
                continue
            act.wait_ge(prep_ready, n + 1)
            if kind in ("ws", "fold"):
                kt = 2 * HALVES + k if kind == "ws" else k
                dst, src = w_hi[:, kt].rearrange("p (b n) -> p b n", b=2), prep_area(n)
            elif kind == "bias":
                dst, src = degw[:].rearrange("p (b n) -> p b n", b=2), prep_area(n)
            else:
                half, c = divmod(k, NC)
                dst, src = state_cols(half, c), ps[:, 2 * (n % 4), 0:CHUNKS[c][1]]
            nc.scalar.copy(dst, src).then_inc(state_ready if kind == "xt" else prep_hi, 1)
        nc.scalar.copy(s_hi[:, 0:FULL], x_nat[:, 0:FULL]).then_inc(s_hi_ready, 1)
        nc.scalar.copy(s_hi[0:LAST, FULL], x_nat[0:LAST, FULL]).then_inc(s_hi_ready, 1)
        act.wait_ge(state_ready, ST0)
        for half in range(HALVES):
            nc.scalar.copy(sc_hi[:, half, 0:CHUNKS[0][1]], state_cols(half, 0)).then_inc(sc_hi_ready, 1)
        act.wait_ge(s_lo_ready, NAT0)
        copy_at(act, nc.scalar.copy, 0, at_act)

        def split_state(i, c, n):
            act.wait_ge(state_ready, n)
            for half in range(HALVES):
                nc.scalar.copy(sc_hi[:, half, 0:CHUNKS[c][1]], state_cols(half, c)).then_inc(sc_hi_ready, 1)

        def turned_hi(i, t):
            act.wait_ge(turned, i * NT + t + 1)
            js = TURNS[t]
            r = ROWS[js[0]]
            nc.scalar.copy(s_hi[0:r, js[0]:js[-1] + 1],
                           ps[0:r, TB, 0:D * len(js)].rearrange("p (t d) -> p t d", d=D)).then_inc(s_hi_ready, 1)

        with act.Fori(0, STEPS) as i:
            turned_hi(i, 0)
            turned_hi(i, 1)
            for c, (c0, cw) in enumerate(CHUNKS):
                base4 = i * 4 * NC + 4 * c
                g0 = i * GATES * NC + GATES * c
                base2 = i * HALVES * NC + HALVES * c
                for q in range(4):
                    act.wait_ge(acc_ready, base4 + q + 1)
                    nc.scalar.copy(a_hi[:, q, 0:cw], ps[:, ACC + q, 0:cw]).then_inc(a_hi_ready, 1)
                for o in range(GATES):
                    g, half = divmod(o, HALVES)
                    buf = (r_buf, z_buf, h_buf)[g]
                    act.wait_ge(gate_ready, g0 + o + 1)
                    if g > 0:
                        act.wait_ge(state_ready, ST0 + base2)
                    nc.scalar.activation(buf[:, half, 0:cw], ps[:, GB + o % 3, 0:cw],
                                         ACT.Tanh if g == 2 else ACT.Sigmoid,
                                         bias=bias[:, o:o + 1]).then_inc(gate_act, 1)
                    if c == NC - 1 and o < 4:
                        turned_hi(i, 2 + o)
                    if g == 0:
                        act.wait_ge(rs_ready, base2 + half + 1)
                        nc.scalar.copy(rs_hi[:, half, 0:cw], r_buf[:, half, 0:cw]).then_inc(rs_hi_ready, 1)
                if c < NC - 1:
                    split_state(i, c + 1, ST0 + i * HALVES * NC)
                else:
                    split_state(i, 0, ST0 + i * HALVES * NC + HALVES)

        act.wait_ge(a_lo_ready, NC + 4 * NC * STEPS)
        for g in range(2):
            act.wait_ge(o_ready, g + 1)
            nc.scalar.copy(o_hi[:, g].rearrange("p k n -> p (k n)"), ps[:, g, :]).then_inc(o_hi_ready, 1)

        def tanh(c):
            cw = CHUNKS[c][1]
            for m in range(HALVES):
                n = HALVES * c + m
                act.wait_ge(t_sum, n + 1)
                if c >= 1:
                    act.wait_ge(t_lo_ready, n - 1)
                if c == 0:
                    act.wait_ge(state_ready, ST0 + HALVES * NC * STEPS)
                nc.scalar.activation(h_buf[:, m, 0:cw], ps[:, GB + n % 3, 0:cw], ACT.Tanh,
                                     bias=bias[:, GATES + m:GATES + m + 1]).then_inc(t_act, 1)
                act.wait_ge(t_act, n + 1)
                if c >= 2:
                    act.wait_ge(y_sum, tiles_of(c - 2)[-1] + 1)
                nc.scalar.copy(end_hidden(c, m)[0], h_buf[:, m, 0:cw]).then_inc(t_hi_ready, 1)

        def end_split(c):
            act.wait_ge(state_ready, ST0 + HALVES * NC * STEPS)
            if c >= 2:
                act.wait_ge(t_sum, HALVES * (c - 1))
            for kt in range(HALVES):
                nc.scalar.copy(end_state(c, kt)[0], state_cols(kt, c)).then_inc(sc_hi_ready, 1)

        end_split(1)
        tanh(0)
        end_split(2)
        tanh(1)
        tanh(2)
        act.wait_ge(eps_ready, 1)
        for c in range(NC):
            ts = tiles_of(c)
            act.wait_ge(mv_ready, ts[-1] + 1)
            full = [t for t in ts if t < FULL]
            nc.scalar.activation(std[:, full[0]:full[-1] + 1], mean_var[:, full[0]:full[-1] + 1, 1], ACT.Sqrt,
                                 bias=eps_col[:, 0:1]).then_inc(std_ready, 1)
        nc.scalar.activation(std[0:LAST, FULL:TILES], mean_var[0:LAST, FULL, 1:2], ACT.Sqrt,
                             bias=eps_col[0:LAST, 0:1]).then_inc(std_ready, 1)

    @block.vector
    def _(dve):
        nc.vector.memset(b_sel[:], 0.0).then_inc(selected, 1)
        nc.vector.memset(e_sel[:].bitcast(F32), 0.0).then_inc(esel_zero, 1)
        dve.wait_ge(small_in, 16 * 6)
        dve.wait_ge(selected, 1)
        for w in range(2):
            for qh in range(HALVES):
                for col in (2 * w, 2 * w + 1):
                    last = nc.vector.tensor_copy(b_sel[:, w * HALVES + qh, col:col + 1],
                                                 io_b[:, w * HALVES + qh:w * HALVES + qh + 1])
        last.then_inc(selected, 1)
        dve.wait_ge(consts, 2)
        for m in range(2):
            last = nc.vector.tensor_tensor(masks[:, m:m + 1], ident[:, m:m + 1], ident[:, m + 2:m + 3], ALU.add)
        last.then_inc(selected, 1)
        dve.wait_ge(esel_zero, 1)
        nc.vector.memset(e_sel[:, 0, 0:2].bitcast(F32), 1.0)
        nc.vector.memset(e_sel[:, 1, 2:4].bitcast(F32), 1.0).then_inc(selected, 1)
        n_hi = 0
        for n, (kind, k) in enumerate(PREP):
            if kind == "xt":
                continue
            dve.wait_ge(prep_ready, n + 1)
            if kind == "wt":
                nc.vector.tensor_copy(wt_f[:, k].rearrange("p (b n) -> p b n", b=2), prep_area(n)).then_inc(prep_out, 1)
                continue
            n_hi += 1
            dve.wait_ge(prep_hi, n_hi)
            if kind in ("ws", "fold"):
                kt = 2 * HALVES + k if kind == "ws" else k
                hi = w_hi[:, kt].rearrange("p (b n) -> p b n", b=2).bitcast(F32)
                nc.vector.tensor_tensor(w_lo[:, kt].rearrange("p (b n) -> p b n", b=2), prep_area(n), hi,
                                        ALU.subtract).then_inc(prep_out, 1)
            else:
                dve.wait_ge(selected, 4)
                nc.vector.tensor_tensor(c_lo[:].rearrange("p (b n) -> p b n", b=2), prep_area(n),
                                        degw[:].rearrange("p (b n) -> p b n", b=2).bitcast(F32),
                                        ALU.subtract).then_inc(c_steps, 1)
                dve.wait_ge(c_steps, 1)
                nc.vector.tensor_scalar(c_lo[:], c_lo[:], masks[:, 1:2], None, ALU.mult).then_inc(c_steps, 1)
                dve.wait_ge(c_steps, 2)
                nc.vector.scalar_tensor_tensor(out=degw[:], in0=degw[:].bitcast(F32), scalar=masks[:, 0:1],
                                               in1=c_lo[:], op0=ALU.mult, op1=ALU.add).then_inc(prep_out, 1)
        dve.wait_ge(s_hi_ready, NAT0)
        nc.vector.tensor_tensor(s_lo[:, 0:FULL], x_nat[:, 0:FULL], s_hi[:, 0:FULL].bitcast(F32),
                                ALU.subtract).then_inc(s_lo_ready, 1)
        nc.vector.tensor_tensor(s_lo[0:LAST, FULL], x_nat[0:LAST, FULL], s_hi[0:LAST, FULL].bitcast(F32),
                                ALU.subtract).then_inc(s_lo_ready, 1)
        for half in range(HALVES):
            dve.wait_ge(sc_hi_ready, half + 1)
            cw = CHUNKS[0][1]
            nc.vector.tensor_tensor(sc_lo[:, half, 0:cw], state_cols(half, 0), sc_hi[:, half, 0:cw].bitcast(F32),
                                    ALU.subtract).then_inc(sc_lo_ready, 1)
        dve.wait_ge(s_lo_ready, NAT0)
        copy_at(dve, nc.vector.tensor_copy, 1, at_dve)
        dve.wait_ge(at_used, TILES)
        for c, (c0, cw) in enumerate(CHUNKS):
            nc.vector.tensor_copy(deg[:, c0:c0 + cw], ps[:, c, 0:cw]).then_inc(a_lo_ready, 1)

        def turned_lo(i, t):
            dve.wait_ge(s_hi_ready, NAT0 + i * NT + t + 1)
            js = TURNS[t]
            r = ROWS[js[0]]
            nc.vector.tensor_tensor(s_lo[0:r, js[0]:js[-1] + 1],
                                    ps[0:r, TB, 0:D * len(js)].rearrange("p (t d) -> p t d", d=D),
                                    s_hi[0:r, js[0]:js[-1] + 1].bitcast(F32),
                                    ALU.subtract).then_inc(s_lo_ready, 1)

        def split_lo(hi, lo, src, n):
            dve.wait_ge(sc_hi_ready, n)
            nc.vector.tensor_tensor(lo, src, hi.bitcast(F32), ALU.subtract).then_inc(sc_lo_ready, 1)

        with dve.Fori(0, STEPS) as i:
            turned_lo(i, 0)
            turned_lo(i, 1)
            for c, (c0, cw) in enumerate(CHUNKS):
                base4 = i * 4 * NC + 4 * c
                g0 = i * GATES * NC + GATES * c
                base2 = i * HALVES * NC + HALVES * c
                for q in range(4):
                    dve.wait_ge(a_hi_ready, base4 + q + 1)
                    nc.vector.tensor_tensor(a_lo[:, q, 0:cw], ps[:, ACC + q, 0:cw], a_hi[:, q, 0:cw].bitcast(F32),
                                            ALU.subtract).then_inc(a_lo_ready, 1)
                for half in range(HALVES):
                    r = r_buf[:, half, 0:cw]
                    dve.wait_ge(gate_act, g0 + half + 1)
                    nc.vector.tensor_tensor(r, r, state_cols(half, c), ALU.mult).then_inc(rs_ready, 1)
                    if c == NC - 1:
                        turned_lo(i, 2 + half)
                    dve.wait_ge(rs_hi_ready, base2 + half + 1)
                    nc.vector.tensor_tensor(rs_lo[:, half, 0:cw], r, rs_hi[:, half, 0:cw].bitcast(F32),
                                            ALU.subtract).then_inc(rs_lo_ready, 1)
                if c == NC - 1:
                    turned_lo(i, 4)
                    turned_lo(i, 5)
                for half in range(HALVES):
                    s, z, h = state_cols(half, c), z_buf[:, half, 0:cw], h_buf[:, half, 0:cw]
                    dve.wait_ge(gate_act, g0 + 2 * HALVES + half + 1)
                    nc.vector.tensor_tensor(h, h, s, ALU.subtract).then_inc(diff_ready, 1)
                    dve.wait_ge(diff_ready, base2 + half + 1)
                    nc.vector.tensor_tensor(h, h, z, ALU.mult).then_inc(zdiff_ready, 1)
                    dve.wait_ge(zdiff_ready, base2 + half + 1)
                    nc.vector.tensor_tensor(s, s, h, ALU.add).then_inc(state_ready, 1)
                nxt = (c + 1) % NC
                w = CHUNKS[nxt][1]
                for half in range(HALVES):
                    split_lo(sc_hi[:, half, 0:w], sc_lo[:, half, 0:w], state_cols(half, nxt),
                             base2 + HALVES + half + 1)

        dve.wait_ge(end_in, 16 * 5)
        for g in range(2):
            dve.wait_ge(o_hi_ready, g + 1)
            nc.vector.tensor_tensor(o_lo[:, g].rearrange("p k n -> p (k n)"), ps[:, g, :],
                                    o_hi[:, g].rearrange("p k n -> p (k n)").bitcast(F32),
                                    ALU.subtract).then_inc(o_lo_ready, 1)
        nc.vector.memset(eps_col[:], EPS).then_inc(eps_ready, 1)

        def end_split_lo(c):
            for kt in range(HALVES):
                hi, lo = end_state(c, kt)
                split_lo(hi, lo, state_cols(kt, c), HALVES * (NC * STEPS + c) + kt + 1)

        def hidden_lo(c):
            for m in range(HALVES):
                hi, lo = end_hidden(c, m)
                dve.wait_ge(t_hi_ready, HALVES * c + m + 1)
                nc.vector.tensor_tensor(lo, h_buf[:, m, 0:CHUNKS[c][1]], hi.bitcast(F32),
                                        ALU.subtract).then_inc(t_lo_ready, 1)

        def rows_out(j):
            r = ROWS[j]
            y = x_end[0:r, j]
            dve.wait_ge(y_sum, j + 1)
            nc.vector.tensor_tensor(y, ps[0:r, ACC + j % 4, 0:D], y, ALU.add).then_inc(y_ready, 1)
            dve.wait_ge(y_ready, j + 1)
            nc.vector.bn_stats(stats[0:r, j], y).then_inc(st_ready, 1)
            dve.wait_ge(st_ready, j + 1)
            nc.vector.bn_aggr(mean_var[0:r, j], stats[0:r, j]).then_inc(mv_ready, 1)

        def normalise(c):
            ts = tiles_of(c)
            full = [t for t in ts if t < FULL]
            dve.wait_ge(std_ready, c + 1)
            nc.vector.reciprocal(rstd[:, full[0]:full[-1] + 1], std[:, full[0]:full[-1] + 1]).then_inc(rstd_ready, 1)
            if c == NC - 1:
                dve.wait_ge(std_ready, NC + 1)
                nc.vector.reciprocal(rstd[0:LAST, FULL:TILES], std[0:LAST, FULL:TILES]).then_inc(rstd_ready, 1)
            dve.wait_ge(rstd_ready, c + 1 + (c == NC - 1))
            for j in ts:
                r = ROWS[j]
                nc.vector.tensor_scalar(x_end[0:r, j], x_end[0:r, j], mean_var[0:r, j, 0:1], rstd[0:r, j:j + 1],
                                        ALU.subtract, ALU.mult).then_inc(normed, 1)

        end_split_lo(1)
        for j in range(TILES):
            nc.vector.tensor_tensor(x_end[0:ROWS[j], j], x_end[0:ROWS[j], j], o_bias[0:ROWS[j]],
                                    ALU.add).then_inc(x_bias, 1)
        hidden_lo(0)
        end_split_lo(2)
        hidden_lo(1)
        dve.wait_ge(x_bias, TILES)
        for j in tiles_of(0):
            rows_out(j)
        hidden_lo(2)
        for j in tiles_of(1):
            rows_out(j)
        normalise(0)
        normalise(1)
        for j in tiles_of(2):
            rows_out(j)
        normalise(2)

    block.__exit__(None, None, None)


_INS = ["x", "adj", "L0_gnn_in_W", "L0_gnn_in_b", "L0_gnn_out_W", "L0_gnn_out_b", "L0_gnn_r_W", "L0_gnn_r_b",
        "L0_gnn_z_W", "L0_gnn_z_b", "L0_gnn_h_W", "L0_gnn_h_b", "L0_gnn_o1_W", "L0_gnn_o1_b", "L0_gnn_o2_W",
        "L0_gnn_o2_b"]


def kernel(**inputs):
    import concourse.bacc as bacc
    from concourse.bass_utils import run_bass_kernel_spmd

    nc = bacc.Bacc("TRN2", target_bir_lowering=False, num_devices=1)
    arrays, args = {}, []
    for name in _INS:
        a = np.ascontiguousarray(inputs[name])
        arrays[f"in_{name}"] = a
        args.append(nc.dram_tensor(f"in_{name}", a.shape, mybir.dt.from_np(a.dtype), kind="ExternalInput").ap())
    shape = inputs["x"].shape
    args.append(nc.dram_tensor("out_0", shape, F32, kind="ExternalOutput").ap())
    gated_graph_network(nc, *args)
    result = run_bass_kernel_spmd(nc, [arrays], core_ids=[0])
    return result.results[0]["out_0"]
```

```python
import numpy as np
import concourse.bass as bass
from concourse import mybir

F32 = mybir.dt.float32
F32R = mybir.dt.float32r
I32 = mybir.dt.int32
ALU = mybir.AluOpType
ACT = mybir.ActivationFunctionType

P = 128
BANK = 512
STEPS = 5
EPS = 1e-5


def gated_graph_network(nc, x, adj, in_W, in_b, out_W, out_b, r_W, r_b, z_W, z_b, h_W, h_b,
                        o1_W, o1_b, o2_W, o2_b, out):
    N, D = x.shape
    HALVES = D // P
    TILES = -(-N // P)
    ROWS = [min(P, N - j * P) for j in range(TILES)]
    CHUNKS = [(c, min(BANK, N - c)) for c in range(0, N, BANK)]
    NC = len(CHUNKS)
    TPC = BANK // P
    GATES = 3 * HALVES
    GW = 3 * D
    KT = 3 * HALVES
    FULL, LAST = TILES - 1, ROWS[-1]
    assert D == 2 * P and NC == 3 and TILES == 11 and FULL == 10

    STREAMED = [5, 6, 7, 8, 9]
    RESIDENT = [j for j in range(TILES) if j not in STREAMED]
    NS, NR = len(STREAMED), len(RESIDENT)

    base = -(-nc.sbuf_base // 32) * 32

    def place(name, shape, dt, at):
        size = int(np.prod(shape[1:])) * 4
        return nc.alloc_sbuf_tensor_at(name, shape, dt, offset=base + at), at + -(-size // 32) * 32

    at = 0
    an_at = at
    an_res, at = place("an_res", [P, NR, N], F32R, at)
    at_res, at = place("at_res", [P, NR, N], F32R, at)
    s_hi, at = place("s_hi", [P, TILES, D], F32R, at)
    slo_at = at
    s_lo, at = place("s_lo", [P, TILES, D], F32R, at)
    w_at = at
    w_hi, at = place("w_hi", [P, KT, GW], F32R, at)
    w_lo, at = place("w_lo", [P, KT, GW], F32R, at)
    deg_at = at
    deg, at = place("deg", [P, N], F32R, at)
    degw, at = place("degw", [P, GW], F32R, at)
    st, at = place("st", [P, HALVES, N], F32, at)
    ring_at = at
    ring_n, at = place("ring_n", [P, NS, BANK], F32R, at)
    ring_t, at = place("ring_t", [P, NS, BANK], F32R, at)
    ident, at = place("ident", [P, P], F32, at)
    bias, at = place("bias", [P, GATES + HALVES], F32, at)
    io_b, at = place("io_b", [P, 2 * HALVES], F32, at)
    masks, at = place("masks", [P, 2], F32, at)
    ident_r, at = place("ident_r", [P, P], F32R, at)
    e_sel, at = place("e_sel", [P, 2, P], F32R, at)
    r_sel, at = place("r_sel", [P, 2, P], F32R, at)
    row_sums, at = place("row_sums", [P, TILES], F32, at)
    o1_hi, at = place("o1_hi", [P, HALVES, D], F32R, at)
    o1_lo, at = place("o1_lo", [P, HALVES, D], F32R, at)
    work_at = at
    a_hi, at = place("a_hi", [P, 4, BANK], F32R, at)
    a_lo, at = place("a_lo", [P, 4, BANK], F32R, at)
    r_buf, at = place("r_buf", [P, HALVES, BANK], F32, at)
    z_buf, at = place("z_buf", [P, HALVES, BANK], F32, at)
    rs_hi, at = place("rs_hi", [P, HALVES, BANK], F32R, at)
    rs_lo, at = place("rs_lo", [P, HALVES, BANK], F32R, at)
    sc_at = at
    sc_hi, at = place("sc_hi", [P, HALVES, BANK], F32R, at)
    sc_lo, at = place("sc_lo", [P, HALVES, BANK], F32R, at)

    def hi_slot(kt):
        return (kt + HALVES) % KT

    w_nat, q = place("w_nat", [P, 3, HALVES, GW], F32, w_at + 4 * HALVES * GW)
    assert q <= w_at + 4 * GW * (KT + 2 * HALVES)
    x_nat, q = place("x_nat", [P, TILES, D], F32, slo_at)
    wt_f, q = place("wt_f", [P, 2 * HALVES, GW], F32, ring_at)
    io_nat, q = place("io_nat", [P, 2, HALVES, D], F32, q)
    b_sel, q = place("b_sel", [P, 2 * HALVES, P], F32, q)
    assert q <= ring_at + 8 * NS * BANK
    o1_nat, q = place("o1_nat", [P, HALVES, D], F32, deg_at)
    c_lo, q = place("c_lo", [P, GW], F32, q)
    assert q <= deg_at + 4 * N
    NI = 3
    a_int, q = place("a_int", [P, NI, N], I32, work_at)
    an_stage, q = place("an_stage", [P, 2, N], F32R, q)
    at_stage, q = place("at_stage", [P, 2, NS, P], F32R, q)
    assert q <= sc_at
    x_end, q = place("x_end", [P, TILES, D], F32, an_at)
    o2_nat, q = place("o2_nat", [P, HALVES, D], F32, q)
    o_bias, q = place("o_bias", [P, D], F32, q)
    o2_hi, q = place("o2_hi", [P, HALVES, D], F32R, q)
    o2_lo, q = place("o2_lo", [P, HALVES, D], F32R, q)
    stats, q = place("stats", [P, TILES, 6], F32, q)
    mean_var, q = place("mean_var", [P, TILES, 2], F32, q)
    std, q = place("std", [P, TILES], F32, q)
    rstd, q = place("rstd", [P, TILES], F32, q)
    shift, q = place("shift", [P, TILES], F32, q)
    eps_col, q = place("eps_col", [P, 1], F32, q)
    assert q <= ring_at

    ps = nc.alloc_psum_tensor("ps", [P, 8, BANK], F32)
    ACC, GB, TB = 0, 4, 7

    far_n = nc.dram_tensor("far_n", [NS, P, N], F32, kind="Internal").ap()
    far_t = nc.dram_tensor("far_t", [NS, P, N], F32, kind="Internal").ap()

    S = nc.alloc_semaphore
    weights_in = S("weights_in")
    proj_in = S("proj_in")
    o1_in = S("o1_in")
    x_in = S("x_in")
    small_in = S("small_in")
    adj_in = [S(f"adj_in{b}") for b in range(NI)]
    consts = S("consts")
    selected = S("selected")
    esel_zero = S("esel_zero")
    ident_r_ready = S("ident_r_ready")
    prep_ready = S("prep_ready")
    prep_act = S("prep_act")
    prep_dve = S("prep_dve")
    c_steps = S("c_steps")
    converted = S("converted")
    at_ready = S("at_ready")
    at_act = S("at_act")
    at_dve = S("at_dve")
    r_sel_ready = S("r_sel_ready")
    row_sums_used = S("row_sums_used")
    far_n_out = [S(f"far_n_out{b}") for b in range(2)]
    far_t_out = [S(f"far_t_out{b}") for b in range(2)]
    streamed_in = [S(f"streamed_in{k}") for k in range(NS)]
    streamed_used = [S(f"streamed_used{k}") for k in range(NS)]
    acc_ready = S("acc_ready")
    a_hi_ready = S("a_hi_ready")
    a_lo_ready = S("a_lo_ready")
    gate_ready = S("gate_ready")
    gate_act = S("gate_act")
    rs_ready = S("rs_ready")
    rs_hi_ready = S("rs_hi_ready")
    rs_lo_ready = S("rs_lo_ready")
    diff_ready = S("diff_ready")
    zdiff_ready = S("zdiff_ready")
    state_ready = S("state_ready")
    sc_hi_ready = S("sc_hi_ready")
    sc_lo_ready = S("sc_lo_ready")
    turned = S("turned")
    s_hi_ready = S("s_hi_ready")
    s_lo_ready = S("s_lo_ready")
    end_in = S("end_in")
    o_ready = S("o_ready")
    o_hi_ready = S("o_hi_ready")
    o_lo_ready = S("o_lo_ready")
    t_sum = S("t_sum")
    t_act = S("t_act")
    t_hi_ready = S("t_hi_ready")
    t_lo_ready = S("t_lo_ready")
    y_sum = S("y_sum")
    x_bias = S("x_bias")
    eps_ready = S("eps_ready")
    y_ready = S("y_ready")
    st_ready = S("st_ready")
    mv_ready = S("mv_ready")
    std_ready = S("std_ready")
    shift_ready = S("shift_ready")
    normed_act = S("normed_act")
    rstd_ready = S("rstd_ready")
    normed = S("normed")
    stored = S("stored")

    def tiles_of(c):
        return range(c * TPC, min((c + 1) * TPC, TILES))

    TURNS = [(8, 9), (10,), (0, 1), (2, 3), (4, 5), (6, 7)]
    NT = len(TURNS)
    NAT0, ST0 = 2, HALVES * NC

    GH = GW // 2
    WT = [("wt", k, b) for k in range(2 * HALVES) for b in range(2)]
    WS = [("ws", k, b) for k in range(HALVES) for b in range(2)]
    FOLD = [("fold", k, b) for k in range(2 * HALVES) for b in range(2)]
    BIAS = [("bias", 0, b) for b in range(2)]
    XT = [("xt", k, 0) for k in range(HALVES * NC)]
    A = [("A", i, 0) for i in range(TILES)]
    PLAN = (A[0:1] + WT + A[1:2] + WS + A[2:3] + FOLD[0:2] + XT[0:3] + A[3:4] + FOLD[2:4] + XT[3:4] + A[4:5]
            + FOLD[4:5] + XT[4:5] + A[5:6] + FOLD[5:6] + XT[5:6] + A[6:7] + FOLD[6:7] + A[7:8] + FOLD[7:8]
            + A[8:9] + BIAS[0:1] + A[9:10] + BIAS[1:2] + [("o1", 0, 0)] + A[10:11])
    PREP = [item for item in PLAN if item[0] != "A"]
    PREP_BANK, AT_BANK = 3, 5

    def prep_dst(n, w=GH):
        return ps[:, PREP_BANK + n % 2, 0:w]

    def on_act(item):
        return item[0] in ("ws", "fold", "bias", "o1") or (item[0] == "wt" and item[2] == 0)

    def on_dve(item):
        return item[0] in ("ws", "fold", "bias", "o1") or (item[0] == "wt" and item[2] == 1)

    def prep_counts(n):
        done = PREP[:n + 1]
        return sum(map(on_act, done)), sum(map(on_dve, done)), sum(1 for k, _, _ in done if k == "xt")

    def wait_prep(eng, n):
        n_act, n_dve, n_xt = prep_counts(n)
        if n_act:
            eng.wait_ge(prep_act, n_act)
        if n_dve:
            eng.wait_ge(prep_dve, n_dve)
        if n_xt:
            eng.wait_ge(state_ready, n_xt)

    AT_GROUPS = [RESIDENT[0:4], [RESIDENT[4], RESIDENT[5], STREAMED[4]], STREAMED[0:4]]
    LAST_XT = max(n for n, item in enumerate(PREP) if item[0] == "xt")

    def an_tile(i):
        return an_res[:, RESIDENT.index(i), :] if i in RESIDENT else an_stage[:, STREAMED.index(i) % 2, :]

    def end_state(c, kt):
        cw = CHUNKS[c][1]
        if c % 2 == 0:
            return sc_hi[:, kt, 0:cw], sc_lo[:, kt, 0:cw]
        return a_hi[:, 2 + kt, 0:cw], a_lo[:, 2 + kt, 0:cw]

    def end_hidden(c, kt):
        cw = CHUNKS[c][1]
        if c % 2 == 0:
            return rs_hi[:, kt, 0:cw], rs_lo[:, kt, 0:cw]
        return a_hi[:, kt, 0:cw], a_lo[:, kt, 0:cw]

    def state_cols(half, c):
        c0, cw = CHUNKS[c]
        return st[:, half, c0:c0 + cw]

    def w_slot(item):
        kind, k, b = item
        kt = 2 * HALVES + k if kind == "ws" else k
        return w_hi[:, hi_slot(kt), b * GH:(b + 1) * GH], w_lo[:, kt, b * GH:(b + 1) * GH]

    block = nc.Block()
    block.__enter__()

    @block.sync
    def _(sp):
        def load_adj(i):
            if i >= NI:
                sp.wait_ge(converted, i - NI + 1)
            sp.dma_start(a_int[0:ROWS[i], i % NI], adj[i * P:i * P + ROWS[i], :]).then_inc(adj_in[i % NI], 16)

        def store_rows(i):
            if i in STREAMED:
                k = STREAMED.index(i)
                sp.wait_ge(converted, i + 1)
                sp.dma_start(far_n[k], an_stage[:, k % 2, :].bitcast(F32)).then_inc(far_n_out[k % 2], 16)

        def store_blocks(i):
            sp.wait_ge(at_dve, 2 * (i + 1))
            sp.dma_start(far_t[:, :, i * P:i * P + ROWS[i]].rearrange("k p n -> p k n"),
                         at_stage[:, i % 2, :, 0:ROWS[i]].bitcast(F32)).then_inc(far_t_out[i % 2], 16)

        load_adj(0)
        for g, w in enumerate((r_W, z_W, h_W)):
            sp.dma_start(w_nat[:, g], w.rearrange("(m p) k -> p m k", p=P)).then_inc(weights_in, 16)
        load_adj(1)
        for g, w in enumerate((in_W, out_W)):
            sp.dma_start(io_nat[:, g], w.rearrange("(m p) k -> p m k", p=P)).then_inc(proj_in, 16)
        load_adj(2)
        sp.dma_start(x_nat[:, 0:FULL], x[0:FULL * P, :].rearrange("(t p) d -> p t d", p=P)).then_inc(x_in, 16)
        sp.dma_start(x_nat[0:LAST, FULL], x[FULL * P:N, :]).then_inc(x_in, 16)
        for i in range(NI, TILES + 3):
            if i < TILES:
                load_adj(i)
            if i == 6:
                sp.dma_start(o1_nat[:], o1_W.rearrange("(m p) k -> p m k", p=P)).then_inc(o1_in, 16)
            if i - 2 < TILES:
                store_rows(i - 2)
            store_blocks(i - 3)
        sp.wait_ge(far_n_out[0], 16 * ((NS + 1) // 2))
        sp.wait_ge(far_n_out[1], 16 * (NS // 2))
        sp.wait_ge(far_t_out[0], 16 * ((TILES + 1) // 2))
        sp.wait_ge(far_t_out[1], 16 * (TILES // 2))

        def stream(c, used):
            c0, cw = CHUNKS[c]
            for k in range(NS):
                if used is not None:
                    sp.wait_ge(streamed_used[k], used)
                sp.dma_start(ring_n[:, k, 0:cw].bitcast(F32), far_n[k, :, c0:c0 + cw]).then_inc(streamed_in[k], 16)
                sp.dma_start(ring_t[:, k, 0:cw].bitcast(F32), far_t[k, :, c0:c0 + cw]).then_inc(streamed_in[k], 16)

        sp.wait_ge(prep_ready, len(PREP))
        stream(0, None)
        with sp.Fori(0, STEPS - 1) as i:
            for c in range(NC):
                stream((c + 1) % NC, i * NC + c + 1)
        for c in range(NC - 1):
            stream(c + 1, (STEPS - 1) * NC + c + 1)
        sp.wait_ge(acc_ready, 4 * NC * STEPS)
        sp.dma_start(o2_nat[:], o2_W.rearrange("(m p) k -> p m k", p=P)).then_inc(end_in, 16)
        sp.dma_start(o_bias[:, :], o2_b.rearrange("(a d) -> a d", a=1).to_broadcast([P, D])).then_inc(end_in, 16)
        sp.dma_start(x_end[:, 0:FULL], x[0:FULL * P, :].rearrange("(t p) d -> p t d", p=P)).then_inc(end_in, 16)
        sp.dma_start(x_end[0:LAST, FULL], x[FULL * P:N, :]).then_inc(end_in, 16)
        for c in range(NC):
            ts = tiles_of(c)
            sp.wait_ge(normed, sum(1 for t in range(ts[-1] + 1) if t % 2 == 0))
            sp.wait_ge(normed_act, sum(1 for t in range(ts[-1] + 1) if t % 2 == 1))
            full = [t for t in ts if t < FULL]
            sp.dma_start(out[full[0] * P:(full[-1] + 1) * P, :].rearrange("(t p) d -> p t d", p=P),
                         x_end[:, full[0]:full[-1] + 1]).then_inc(stored, 16)
        sp.dma_start(out[FULL * P:N, :], x_end[0:LAST, FULL]).then_inc(stored, 16)
        sp.wait_ge(stored, 16 * (NC + 1))

    @block.gpsimd
    def _(pool):
        nc.gpsimd.memset(ident[:], 0.0).then_inc(consts, 1)
        pool.wait_ge(consts, 1)
        nc.gpsimd.affine_select(out=ident[:], in_=ident[:], compare_op=ALU.not_equal, fill=1.0, base=0,
                                pattern=[[-1, P]], channel_multiplier=1).then_inc(consts, 1)
        pool.wait_ge(end_in, 16 * 4)
        nc.gpsimd.tensor_tensor(x_end[:, 0:FULL], x_end[:, 0:FULL],
                                o_bias[:].unsqueeze(1).to_broadcast([P, FULL, D]), ALU.add).then_inc(x_bias, 1)
        nc.gpsimd.tensor_tensor(x_end[0:LAST, FULL], x_end[0:LAST, FULL], o_bias[0:LAST], ALU.add).then_inc(x_bias, 1)

    @block.tensor
    def _(pe):
        def three(dst, kt, cols, hi, lo, start, stop, wh=w_hi, wl=w_lo):
            ks = hi_slot(kt) if wh is w_hi else kt
            nc.tensor.matmul(dst, wh[:, ks, cols], hi, start=start, stop=False)
            nc.tensor.matmul(dst, wh[:, ks, cols], lo, start=False, stop=False)
            return nc.tensor.matmul(dst, wl[:, kt, cols], hi, start=False, stop=stop)

        def weight_bank(n, item):
            kind, k, b = item
            if n >= 2:
                wait_prep(pe, n - 2)
            dst = prep_dst(n)
            if kind in ("wt", "ws"):
                qt = k if kind == "wt" else 2 * HALVES + k
                for o in range(3 * b, 3 * b + 3):
                    g, m = divmod(o, HALVES)
                    last = nc.tensor.transpose(dst[:, (o % 3) * P:(o % 3 + 1) * P],
                                               w_nat[:, g, m, qt * P:(qt + 1) * P], ident[:])
            elif kind == "fold":
                which, kt = divmod(k, HALVES)
                for qh in range(HALVES):
                    last = nc.tensor.matmul(dst, io_nat[:, which, qh, kt * P:(kt + 1) * P],
                                            wt_f[:, which * HALVES + qh, b * GH:(b + 1) * GH],
                                            start=(qh == 0), stop=(qh == HALVES - 1))
            elif kind == "bias":
                for qt in range(2 * HALVES):
                    last = nc.tensor.matmul(dst, b_sel[:, qt], wt_f[:, qt, b * GH:(b + 1) * GH],
                                            start=(qt == 0), stop=(qt == 2 * HALVES - 1))
            elif kind == "xt":
                half, c = divmod(k, NC)
                for j in tiles_of(c):
                    r = ROWS[j]
                    last = nc.tensor.transpose(prep_dst(n, BANK)[:, (j % TPC) * P:(j % TPC) * P + r],
                                               x_nat[0:r, j, half * P:(half + 1) * P], ident[0:r, 0:r])
            else:
                for kt in range(HALVES):
                    for m in range(HALVES):
                        last = nc.tensor.transpose(prep_dst(n, BANK)[:, kt * D + m * P:kt * D + (m + 1) * P],
                                                   o1_nat[:, m, kt * P:(kt + 1) * P], ident[:])
            last.then_inc(prep_ready, 1)

        def adjacency_tile(i):
            r, tile = ROWS[i], an_tile(i)
            pe.wait_ge(converted, i + 1)
            for c, (c0, cw) in enumerate(CHUNKS):
                nc.tensor.matmul(ps[:, c, 0:cw], e_sel[0:r, 1], tile[0:r, c0:c0 + cw],
                                 start=(i == 0), stop=False, skip_group_check=True)
            for g, group in enumerate(AT_GROUPS):
                if i > 0:
                    if g == 0:
                        pe.wait_ge(at_act, i)
                    else:
                        pe.wait_ge(at_dve, 2 * (i - 1) + g)
                for k, j in enumerate(group):
                    last = nc.tensor.matmul(ps[0:ROWS[j], AT_BANK + g, k * P:k * P + r],
                                            tile[0:r, j * P:j * P + ROWS[j]], ident_r[0:r, 0:r],
                                            start=True, stop=True)
                last.then_inc(at_ready, 1)
            c, off = divmod(i, TPC)
            pe.wait_ge(r_sel_ready, i + 1)
            nc.tensor.matmul(ps[:, c, off * P:off * P + r], r_sel[0:r, i % 2], ident_r[0:r, 0:r], start=False,
                             stop=(i == TILES - 1), skip_group_check=True).then_inc(row_sums_used, 1)

        pe.wait_ge(consts, 2)
        pe.wait_ge(ident_r_ready, 1)
        pe.wait_ge(selected, 4)
        arrivals = {"wt": (weights_in, 16 * 3), "fold": (proj_in, 16 * 2), "xt": (x_in, 16 * 2), "o1": (o1_in, 16)}
        n = 0
        for item in PLAN:
            kind, k, b = item
            if kind in arrivals and k == 0 and b == 0:
                pe.wait_ge(*arrivals[kind])
            if kind == "A":
                adjacency_tile(k)
            else:
                weight_bank(n, item)
                n += 1
        wait_prep(pe, len(PREP) - 1)
        pe.wait_ge(at_act, TILES)
        pe.wait_ge(at_dve, 2 * TILES)
        pe.wait_ge(a_lo_ready, NC)

        def turn(i, t):
            pe.wait_ge(s_lo_ready, NAT0 + i * NT + t)
            for n, j in enumerate(TURNS[t]):
                for half in range(HALVES):
                    last = nc.tensor.transpose(ps[0:ROWS[j], TB, n * D + half * P:n * D + (half + 1) * P],
                                               st[:, half, j * P:j * P + ROWS[j]], ident[:])
            last.then_inc(turned, 1)

        def aggregate(i, c):
            c0, cw = CHUNKS[c]
            pe.wait_ge(a_lo_ready, NC + i * 4 * NC + 4 * c)
            if c == 0:
                pe.wait_ge(s_hi_ready, NAT0 + i * NT)
                pe.wait_ge(s_lo_ready, NAT0 + i * NT)
            for j in range(TILES):
                r = ROWS[j]
                if c == 0 and j == 6:
                    pe.wait_ge(state_ready, ST0 + i * NC * HALVES)
                    turn(i, 0)
                if c == 0 and j == 7:
                    turn(i, 1)
                if c == 0 and j == TURNS[0][0]:
                    pe.wait_ge(s_hi_ready, NAT0 + i * NT + 1)
                    pe.wait_ge(s_lo_ready, NAT0 + i * NT + 1)
                if c == 0 and j == TURNS[1][0]:
                    pe.wait_ge(s_hi_ready, NAT0 + i * NT + 2)
                    pe.wait_ge(s_lo_ready, NAT0 + i * NT + 2)
                if j in STREAMED:
                    k = STREAMED.index(j)
                    pe.wait_ge(streamed_in[k], i * 32 * NC + 32 * (c + 1))
                    rows_t, rows_n = ring_t[0:r, k, 0:cw], ring_n[0:r, k, 0:cw]
                else:
                    k = RESIDENT.index(j)
                    rows_t, rows_n = at_res[0:r, k, c0:c0 + cw], an_res[0:r, k, c0:c0 + cw]
                for q in range(4):
                    rows, half = (rows_t, rows_n)[q // HALVES], q % HALVES
                    dst = ps[:, ACC + q, 0:cw]
                    nc.tensor.matmul(dst, s_hi[0:r, j, half * P:(half + 1) * P], rows, start=(j == 0), stop=False)
                    last = nc.tensor.matmul(dst, s_lo[0:r, j, half * P:(half + 1) * P], rows, start=False,
                                            stop=(j == TILES - 1))
                    if j == TILES - 1:
                        last.then_inc(acc_ready, 1)
                if j in STREAMED:
                    last.then_inc(streamed_used[STREAMED.index(j)], 1)

        def gates(i, c):
            c0, cw = CHUNKS[c]
            g0 = i * GATES * NC + GATES * c
            base4 = i * 4 * NC + 4 * c
            base2 = i * HALVES * NC + HALVES * c

            def dst(o):
                return ps[:, GB + o % 3, 0:cw]

            def state_part(o):
                for half in range(HALVES):
                    three(dst(o), 2 * HALVES + half, slice(o * P, (o + 1) * P),
                          sc_hi[:, half, 0:cw], sc_lo[:, half, 0:cw], half == 0, False)

            def degree_part(o, start):
                nc.tensor.matmul(dst(o), degw[:, o * P:(o + 1) * P], deg[:, c0:c0 + cw], start=start, stop=False)

            def sums_part(o, stop):
                for q in range(4):
                    if o == 0:
                        pe.wait_ge(a_hi_ready, base4 + q + 1)
                        pe.wait_ge(a_lo_ready, NC + base4 + q + 1)
                    last = three(dst(o), q, slice(o * P, (o + 1) * P), a_hi[:, q, 0:cw], a_lo[:, q, 0:cw],
                                 False, stop and q == 3)
                return last

            if c > 0:
                pe.wait_ge(gate_act, g0)
            pe.wait_ge(sc_hi_ready, base2 + HALVES)
            pe.wait_ge(sc_lo_ready, base2 + HALVES)
            for o in range(3):
                state_part(o)
                degree_part(o, False)
            for o in range(4):
                if o == 3:
                    pe.wait_ge(gate_act, g0 + 1)
                    state_part(o)
                    degree_part(o, False)
                sums_part(o, True).then_inc(gate_ready, 1)
                if c == NC - 1:
                    turn(i, 2 + o)
            for o in range(4, GATES):
                pe.wait_ge(gate_act, g0 + o - 2)
                degree_part(o, True)
                sums_part(o, False)
                for half in range(HALVES):
                    if o == 4:
                        pe.wait_ge(rs_hi_ready, base2 + half + 1)
                        pe.wait_ge(rs_lo_ready, base2 + half + 1)
                    last = three(dst(o), 2 * HALVES + half, slice(o * P, (o + 1) * P),
                                 rs_hi[:, half, 0:cw], rs_lo[:, half, 0:cw], False, half == HALVES - 1)
                last.then_inc(gate_ready, 1)

        with pe.Fori(0, STEPS) as i:
            for c in range(NC):
                aggregate(i, c)
                gates(i, c)

        def hidden(c):
            cw = CHUNKS[c][1]
            n_sc = HALVES * (NC * STEPS + c + 1)
            pe.wait_ge(sc_hi_ready, n_sc)
            pe.wait_ge(sc_lo_ready, n_sc)
            for m in range(HALVES):
                n = HALVES * c + m
                if n >= 3:
                    pe.wait_ge(t_act, n - 2)
                elif n > 0:
                    pe.wait_ge(gate_act, GATES * NC * STEPS - 2 + n)
                dst = ps[:, GB + n % 3, 0:cw]
                for kt in range(HALVES):
                    hi, lo = end_state(c, kt)
                    last = three(dst, 0, slice(m * P, (m + 1) * P), hi, lo, kt == 0, kt == HALVES - 1,
                                 o1_hi[:, kt:kt + 1], o1_lo[:, kt:kt + 1])
                last.then_inc(t_sum, 1)

        def head(c):
            pe.wait_ge(t_hi_ready, HALVES * (c + 1))
            pe.wait_ge(t_lo_ready, HALVES * (c + 1))
            for j in tiles_of(c):
                r = ROWS[j]
                if j >= 4:
                    pe.wait_ge(y_ready, j - 3)
                dst = ps[0:r, ACC + j % 4, 0:D]
                off = (j % TPC) * P
                for kt in range(HALVES):
                    hi, lo = end_hidden(c, kt)
                    hi, lo = hi[:, off:off + r], lo[:, off:off + r]
                    nc.tensor.matmul(dst, hi, o2_hi[:, kt], start=(kt == 0), stop=False)
                    nc.tensor.matmul(dst, hi, o2_lo[:, kt], start=False, stop=False)
                    last = nc.tensor.matmul(dst, lo, o2_hi[:, kt], start=False, stop=(kt == HALVES - 1))
                last.then_inc(y_sum, 1)

        pe.wait_ge(gate_act, GATES * NC * STEPS - 2)
        hidden(0)
        pe.wait_ge(end_in, 16 * 4)
        for kt in range(HALVES):
            for m in range(HALVES):
                last = nc.tensor.transpose(ps[:, TB, kt * D + m * P:kt * D + (m + 1) * P],
                                           o2_nat[:, m, kt * P:(kt + 1) * P], ident[:])
        last.then_inc(o_ready, 1)
        hidden(1)
        pe.wait_ge(o_hi_ready, 1)
        pe.wait_ge(o_lo_ready, 1)
        head(0)
        hidden(2)
        head(1)
        head(2)

    @block.scalar
    def _(act):
        for n, b in enumerate((r_b, z_b, h_b, o1_b)):
            act.dma_start(bias[:, n * HALVES:(n + 1) * HALVES],
                          b.rearrange("(m p) -> p m", p=P),
                          allow_slow_non_contiguous=True).then_inc(small_in, 16)
        for n, b in enumerate((in_b, out_b)):
            act.dma_start(io_b[:, n * HALVES:(n + 1) * HALVES],
                          b.rearrange("(m p) -> p m", p=P),
                          allow_slow_non_contiguous=True).then_inc(small_in, 16)
        act.wait_ge(consts, 2)
        nc.scalar.copy(ident_r[:], ident[:]).then_inc(ident_r_ready, 1)

        def convert(i):
            act.wait_ge(adj_in[i % NI], 16 * (i // NI + 1))
            if i in STREAMED and STREAMED.index(i) >= 2:
                k = STREAMED.index(i)
                act.wait_ge(at_ready, 3 * (i - 1))
                act.wait_ge(far_n_out[k % 2], 16 * (k // 2))
            r = ROWS[i]
            nc.scalar.activation(an_tile(i)[0:r], a_int[0:r, i % NI], ACT.Copy,
                                 accum_out=row_sums[0:r, i:i + 1]).then_inc(converted, 1)

        convert(0)
        n = 0
        for item in PLAN:
            kind, k, b = item
            if kind == "A":
                if k + 1 < TILES:
                    convert(k + 1)
                act.wait_ge(at_ready, 3 * k + 1)
                r = ROWS[k]
                nc.scalar.copy(at_res[:, 0:4, k * P:k * P + r],
                               ps[:, AT_BANK].rearrange("p (k n) -> p k n", k=4)[:, :, 0:r]).then_inc(at_act, 1)
                continue
            if kind == "xt":
                half, c = divmod(k, NC)
                act.wait_ge(prep_ready, n + 1)
                nc.scalar.copy(state_cols(half, c), prep_dst(n, CHUNKS[c][1])).then_inc(state_ready, 1)
            elif on_act(item):
                act.wait_ge(prep_ready, n + 1)
                if kind == "wt":
                    dst, src = wt_f[:, k, b * GH:(b + 1) * GH], prep_dst(n)
                elif kind == "bias":
                    dst, src = degw[:, b * GH:(b + 1) * GH], prep_dst(n)
                elif kind == "o1":
                    dst, src = o1_hi[:].rearrange("p k n -> p (k n)"), prep_dst(n, BANK)
                else:
                    dst, src = w_slot(item)[0], prep_dst(n)
                nc.scalar.copy(dst, src).then_inc(prep_act, 1)
            if item == XT[-1]:
                nc.scalar.copy(s_hi[:, 0:FULL], x_nat[:, 0:FULL]).then_inc(s_hi_ready, 1)
                nc.scalar.copy(s_hi[0:LAST, FULL], x_nat[0:LAST, FULL]).then_inc(s_hi_ready, 1)
                act.wait_ge(state_ready, ST0)
                for half in range(HALVES):
                    nc.scalar.copy(sc_hi[:, half, 0:CHUNKS[0][1]], state_cols(half, 0)).then_inc(sc_hi_ready, 1)
            n += 1

        def split_state(i, c, n):
            act.wait_ge(state_ready, n)
            for half in range(HALVES):
                nc.scalar.copy(sc_hi[:, half, 0:CHUNKS[c][1]], state_cols(half, c)).then_inc(sc_hi_ready, 1)

        def turned_hi(i, t):
            act.wait_ge(turned, i * NT + t + 1)
            js = TURNS[t]
            r = ROWS[js[0]]
            nc.scalar.copy(s_hi[0:r, js[0]:js[-1] + 1],
                           ps[0:r, TB, 0:D * len(js)].rearrange("p (t d) -> p t d", d=D)).then_inc(s_hi_ready, 1)

        with act.Fori(0, STEPS) as i:
            turned_hi(i, 0)
            turned_hi(i, 1)
            for c, (c0, cw) in enumerate(CHUNKS):
                base4 = i * 4 * NC + 4 * c
                g0 = i * GATES * NC + GATES * c
                base2 = i * HALVES * NC + HALVES * c
                for q in range(4):
                    act.wait_ge(acc_ready, base4 + q + 1)
                    nc.scalar.copy(a_hi[:, q, 0:cw], ps[:, ACC + q, 0:cw]).then_inc(a_hi_ready, 1)
                for o in range(GATES):
                    g, half = divmod(o, HALVES)
                    buf = (r_buf, z_buf, r_buf)[g]
                    if o == 0:
                        act.wait_ge(state_ready, ST0 + base2)
                    act.wait_ge(gate_ready, g0 + o + 1)
                    nc.scalar.activation(buf[:, half, 0:cw], ps[:, GB + o % 3, 0:cw],
                                         ACT.Tanh if g == 2 else ACT.Sigmoid,
                                         bias=bias[:, o:o + 1]).then_inc(gate_act, 1)
                    if c == NC - 1 and o < 4:
                        turned_hi(i, 2 + o)
                    if g == 0:
                        act.wait_ge(rs_ready, base2 + half + 1)
                        nc.scalar.copy(rs_hi[:, half, 0:cw], r_buf[:, half, 0:cw]).then_inc(rs_hi_ready, 1)
                    if o == 2 * HALVES - 1:
                        if c < NC - 1:
                            split_state(i, c + 1, ST0 + i * HALVES * NC)
                        else:
                            split_state(i, 0, ST0 + i * HALVES * NC + HALVES)

        def tanh(c):
            cw = CHUNKS[c][1]
            for m in range(HALVES):
                n = HALVES * c + m
                act.wait_ge(t_sum, n + 1)
                if c >= 1:
                    act.wait_ge(t_lo_ready, n - 1)
                if c == 0:
                    act.wait_ge(state_ready, ST0 + HALVES * NC * STEPS)
                nc.scalar.activation(z_buf[:, m, 0:cw], ps[:, GB + n % 3, 0:cw], ACT.Tanh,
                                     bias=bias[:, GATES + m:GATES + m + 1]).then_inc(t_act, 1)
                act.wait_ge(t_act, n + 1)
                if c >= 2:
                    act.wait_ge(y_sum, tiles_of(c - 2)[-1] + 1)
                nc.scalar.copy(end_hidden(c, m)[0], z_buf[:, m, 0:cw]).then_inc(t_hi_ready, 1)

        def end_split(c):
            act.wait_ge(state_ready, ST0 + HALVES * NC * STEPS)
            if c >= 2:
                act.wait_ge(t_sum, HALVES * (c - 1))
            for kt in range(HALVES):
                nc.scalar.copy(end_state(c, kt)[0], state_cols(kt, c)).then_inc(sc_hi_ready, 1)

        end_split(1)
        tanh(0)
        act.wait_ge(o_ready, 1)
        nc.scalar.copy(o2_hi[:].rearrange("p k n -> p (k n)"), ps[:, TB, :]).then_inc(o_hi_ready, 1)
        end_split(2)
        tanh(1)
        tanh(2)
        act.wait_ge(eps_ready, 1)
        for c in range(NC):
            ts = tiles_of(c)
            act.wait_ge(mv_ready, ts[-1] + 1)
            full = [t for t in ts if t < FULL]
            nc.scalar.activation(std[:, full[0]:full[-1] + 1], mean_var[:, full[0]:full[-1] + 1, 1], ACT.Sqrt,
                                 bias=eps_col[:, 0:1]).then_inc(std_ready, 1)
            if c == NC - 1:
                nc.scalar.activation(std[0:LAST, FULL:TILES], mean_var[0:LAST, FULL, 1:2], ACT.Sqrt,
                                     bias=eps_col[0:LAST, 0:1]).then_inc(std_ready, 1)
            act.wait_ge(shift_ready, c + 1 + (c == NC - 1))
            for j in ts:
                if j % 2 == 1:
                    nc.scalar.activation(x_end[:, j], x_end[:, j], ACT.Identity, bias=shift[:, j:j + 1],
                                         scale=rstd[:, j:j + 1]).then_inc(normed_act, 1)

    @block.vector
    def _(dve):
        nc.vector.memset(b_sel[:], 0.0).then_inc(selected, 1)
        nc.vector.memset(e_sel[:].bitcast(F32), 0.0).then_inc(esel_zero, 1)
        dve.wait_ge(small_in, 16 * 6)
        dve.wait_ge(selected, 1)
        for w in range(2):
            for qh in range(HALVES):
                for col in (2 * w, 2 * w + 1):
                    last = nc.vector.tensor_copy(b_sel[:, w * HALVES + qh, col:col + 1],
                                                 io_b[:, w * HALVES + qh:w * HALVES + qh + 1])
        last.then_inc(selected, 1)
        dve.wait_ge(consts, 2)
        for m in range(2):
            last = nc.vector.tensor_tensor(masks[:, m:m + 1], ident[:, m:m + 1], ident[:, m + 2:m + 3], ALU.add)
        last.then_inc(selected, 1)
        dve.wait_ge(esel_zero, 1)
        nc.vector.memset(e_sel[:, 0, 0:2].bitcast(F32), 1.0)
        nc.vector.memset(e_sel[:, 1, 2:4].bitcast(F32), 1.0).then_inc(selected, 1)
        n = 0
        for item in PLAN:
            kind, k, b = item
            if kind == "A":
                r = ROWS[k]
                dve.wait_ge(converted, k + 1)
                dve.wait_ge(selected, 4)
                if k >= 2:
                    dve.wait_ge(row_sums_used, k - 1)
                nc.vector.tensor_scalar(r_sel[0:r, k % 2], e_sel[0:r, 0].bitcast(F32), row_sums[0:r, k:k + 1], None,
                                        ALU.mult).then_inc(r_sel_ready, 1)
                if k >= 2:
                    dve.wait_ge(far_t_out[k % 2], 16 * (k // 2))
                dve.wait_ge(at_ready, 3 * k + 2)
                b1 = ps[:, AT_BANK + 1]
                nc.vector.tensor_copy(at_res[:, 4, k * P:k * P + r], b1[:, 0:r])
                nc.vector.tensor_copy(at_res[0:LAST, 5, k * P:k * P + r], b1[0:LAST, P:P + r])
                nc.vector.tensor_copy(at_stage[:, k % 2, 4, 0:r], b1[:, 2 * P:2 * P + r]).then_inc(at_dve, 1)
                dve.wait_ge(at_ready, 3 * k + 3)
                nc.vector.tensor_copy(at_stage[:, k % 2, 0:4, 0:r],
                                      ps[:, AT_BANK + 2].rearrange("p (k n) -> p k n", k=4)[:, :, 0:r]
                                      ).then_inc(at_dve, 1)
                continue
            if on_dve(item):
                dve.wait_ge(prep_ready, n + 1)
                if kind == "wt":
                    nc.vector.tensor_copy(wt_f[:, k, b * GH:(b + 1) * GH], prep_dst(n)).then_inc(prep_dve, 1)
                else:
                    dve.wait_ge(prep_act, prep_counts(n)[0])
                    if kind == "bias":
                        cols = slice(b * GH, (b + 1) * GH)
                        nc.vector.tensor_tensor(c_lo[:, cols], prep_dst(n), degw[:, cols].bitcast(F32),
                                                ALU.subtract).then_inc(c_steps, 1)
                        dve.wait_ge(c_steps, 2 * b + 1)
                        nc.vector.tensor_scalar(c_lo[:, cols], c_lo[:, cols], masks[:, 1:2], None,
                                                ALU.mult).then_inc(c_steps, 1)
                        dve.wait_ge(c_steps, 2 * b + 2)
                        nc.vector.scalar_tensor_tensor(out=degw[:, cols], in0=degw[:, cols].bitcast(F32),
                                                       scalar=masks[:, 0:1], in1=c_lo[:, cols],
                                                       op0=ALU.mult, op1=ALU.add).then_inc(prep_dve, 1)
                    elif kind == "o1":
                        hi = o1_hi[:].rearrange("p k n -> p (k n)")
                        nc.vector.tensor_tensor(o1_lo[:].rearrange("p k n -> p (k n)"), prep_dst(n, BANK),
                                                hi.bitcast(F32), ALU.subtract).then_inc(prep_dve, 1)
                    else:
                        hi, lo = w_slot(item)
                        nc.vector.tensor_tensor(lo, prep_dst(n), hi.bitcast(F32), ALU.subtract).then_inc(prep_dve, 1)
            if item == XT[-1]:
                dve.wait_ge(prep_ready, n + 1)
                dve.wait_ge(s_hi_ready, NAT0)
                nc.vector.tensor_tensor(s_lo[:, 0:FULL], x_nat[:, 0:FULL], s_hi[:, 0:FULL].bitcast(F32),
                                        ALU.subtract).then_inc(s_lo_ready, 1)
                nc.vector.tensor_tensor(s_lo[0:LAST, FULL], x_nat[0:LAST, FULL], s_hi[0:LAST, FULL].bitcast(F32),
                                        ALU.subtract).then_inc(s_lo_ready, 1)
                for half in range(HALVES):
                    cw = CHUNKS[0][1]
                    dve.wait_ge(sc_hi_ready, half + 1)
                    nc.vector.tensor_tensor(sc_lo[:, half, 0:cw], state_cols(half, 0),
                                            sc_hi[:, half, 0:cw].bitcast(F32), ALU.subtract).then_inc(sc_lo_ready, 1)
            n += 1
        dve.wait_ge(row_sums_used, TILES)
        dve.wait_ge(prep_dve, prep_counts(len(PREP) - 1)[1])
        for c, (c0, cw) in enumerate(CHUNKS):
            nc.vector.tensor_copy(deg[:, c0:c0 + cw], ps[:, c, 0:cw]).then_inc(a_lo_ready, 1)

        def turned_lo(i, t):
            dve.wait_ge(s_hi_ready, NAT0 + i * NT + t + 1)
            js = TURNS[t]
            r = ROWS[js[0]]
            nc.vector.tensor_tensor(s_lo[0:r, js[0]:js[-1] + 1],
                                    ps[0:r, TB, 0:D * len(js)].rearrange("p (t d) -> p t d", d=D),
                                    s_hi[0:r, js[0]:js[-1] + 1].bitcast(F32),
                                    ALU.subtract).then_inc(s_lo_ready, 1)

        def split_lo(hi, lo, src, n):
            dve.wait_ge(sc_hi_ready, n)
            nc.vector.tensor_tensor(lo, src, hi.bitcast(F32), ALU.subtract).then_inc(sc_lo_ready, 1)

        with dve.Fori(0, STEPS) as i:
            turned_lo(i, 0)
            turned_lo(i, 1)
            for c, (c0, cw) in enumerate(CHUNKS):
                base4 = i * 4 * NC + 4 * c
                g0 = i * GATES * NC + GATES * c
                base2 = i * HALVES * NC + HALVES * c
                for q in range(4):
                    dve.wait_ge(a_hi_ready, base4 + q + 1)
                    nc.vector.tensor_tensor(a_lo[:, q, 0:cw], ps[:, ACC + q, 0:cw], a_hi[:, q, 0:cw].bitcast(F32),
                                            ALU.subtract).then_inc(a_lo_ready, 1)
                for half in range(HALVES):
                    r = r_buf[:, half, 0:cw]
                    dve.wait_ge(gate_act, g0 + half + 1)
                    nc.vector.tensor_tensor(r, r, state_cols(half, c), ALU.mult).then_inc(rs_ready, 1)
                    if c == NC - 1:
                        turned_lo(i, 2 + half)
                    dve.wait_ge(rs_hi_ready, base2 + half + 1)
                    nc.vector.tensor_tensor(rs_lo[:, half, 0:cw], r, rs_hi[:, half, 0:cw].bitcast(F32),
                                            ALU.subtract).then_inc(rs_lo_ready, 1)
                if c == NC - 1:
                    turned_lo(i, 4)
                    turned_lo(i, 5)
                nxt = (c + 1) % NC
                w = CHUNKS[nxt][1]
                for half in range(HALVES):
                    split_lo(sc_hi[:, half, 0:w], sc_lo[:, half, 0:w], state_cols(half, nxt),
                             base2 + HALVES + half + 1)
                for half in range(HALVES):
                    s, z, h = state_cols(half, c), z_buf[:, half, 0:cw], r_buf[:, half, 0:cw]
                    dve.wait_ge(gate_act, g0 + 2 * HALVES + half + 1)
                    nc.vector.tensor_tensor(h, h, s, ALU.subtract).then_inc(diff_ready, 1)
                    dve.wait_ge(diff_ready, base2 + half + 1)
                    nc.vector.tensor_tensor(h, h, z, ALU.mult).then_inc(zdiff_ready, 1)
                    dve.wait_ge(zdiff_ready, base2 + half + 1)
                    nc.vector.tensor_tensor(s, s, h, ALU.add).then_inc(state_ready, 1)

        dve.wait_ge(end_in, 16 * 4)
        nc.vector.memset(eps_col[:], EPS).then_inc(eps_ready, 1)

        def o2_low():
            dve.wait_ge(o_hi_ready, 1)
            nc.vector.tensor_tensor(o2_lo[:].rearrange("p k n -> p (k n)"), ps[:, TB, :],
                                    o2_hi[:].rearrange("p k n -> p (k n)").bitcast(F32),
                                    ALU.subtract).then_inc(o_lo_ready, 1)

        def end_split_lo(c):
            for kt in range(HALVES):
                hi, lo = end_state(c, kt)
                split_lo(hi, lo, state_cols(kt, c), HALVES * (NC * STEPS + c) + kt + 1)

        def hidden_lo(c):
            for m in range(HALVES):
                hi, lo = end_hidden(c, m)
                dve.wait_ge(t_hi_ready, HALVES * c + m + 1)
                nc.vector.tensor_tensor(lo, z_buf[:, m, 0:CHUNKS[c][1]], hi.bitcast(F32),
                                        ALU.subtract).then_inc(t_lo_ready, 1)

        def rows_out(js):
            for n in range(len(js) + 2):
                if n < len(js):
                    j = js[n]
                    y = x_end[0:ROWS[j], j]
                    dve.wait_ge(y_sum, j + 1)
                    nc.vector.tensor_tensor(y, ps[0:ROWS[j], ACC + j % 4, 0:D], y, ALU.add).then_inc(y_ready, 1)
                if 1 <= n < len(js) + 1:
                    j = js[n - 1]
                    dve.wait_ge(y_ready, j + 1)
                    nc.vector.bn_stats(stats[0:ROWS[j], j], x_end[0:ROWS[j], j]).then_inc(st_ready, 1)
                if n >= 2:
                    j = js[n - 2]
                    dve.wait_ge(st_ready, j + 1)
                    nc.vector.bn_aggr(mean_var[0:ROWS[j], j], stats[0:ROWS[j], j]).then_inc(mv_ready, 1)

        def normalise(c):
            ts = tiles_of(c)
            full = [t for t in ts if t < FULL]
            parts = [(P, full[0], full[-1] + 1)] + ([(LAST, FULL, TILES)] if c == NC - 1 else [])
            for n, (r, a, b) in enumerate(parts):
                dve.wait_ge(std_ready, c + n + 1)
                nc.vector.reciprocal(rstd[0:r, a:b], std[0:r, a:b]).then_inc(rstd_ready, 1)
            for n, (r, a, b) in enumerate(parts):
                dve.wait_ge(rstd_ready, c + n + 1)
                nc.vector.scalar_tensor_tensor(out=shift[0:r, a:b], in0=mean_var[0:r, a:b, 0], scalar=-1.0,
                                               in1=rstd[0:r, a:b], op0=ALU.mult, op1=ALU.mult).then_inc(shift_ready, 1)
            for j in ts:
                if j % 2 == 0:
                    r = ROWS[j]
                    nc.vector.tensor_scalar(x_end[0:r, j], x_end[0:r, j], mean_var[0:r, j, 0:1], rstd[0:r, j:j + 1],
                                            ALU.subtract, ALU.mult).then_inc(normed, 1)

        end_split_lo(1)
        hidden_lo(0)
        o2_low()
        end_split_lo(2)
        hidden_lo(1)
        dve.wait_ge(x_bias, 2)
        rows_out(tiles_of(0))
        hidden_lo(2)
        rows_out(tiles_of(1))
        normalise(0)
        rows_out(tiles_of(2))
        normalise(1)
        normalise(2)

    block.__exit__(None, None, None)


_INS = ["x", "adj", "L0_gnn_in_W", "L0_gnn_in_b", "L0_gnn_out_W", "L0_gnn_out_b", "L0_gnn_r_W", "L0_gnn_r_b",
        "L0_gnn_z_W", "L0_gnn_z_b", "L0_gnn_h_W", "L0_gnn_h_b", "L0_gnn_o1_W", "L0_gnn_o1_b", "L0_gnn_o2_W",
        "L0_gnn_o2_b"]


def kernel(**inputs):
    import concourse.bacc as bacc
    from concourse.bass_utils import run_bass_kernel_spmd

    nc = bacc.Bacc("TRN2", target_bir_lowering=False, num_devices=1)
    arrays, args = {}, []
    for name in _INS:
        a = np.ascontiguousarray(inputs[name])
        arrays[f"in_{name}"] = a
        args.append(nc.dram_tensor(f"in_{name}", a.shape, mybir.dt.from_np(a.dtype), kind="ExternalInput").ap())
    shape = inputs["x"].shape
    args.append(nc.dram_tensor("out_0", shape, F32, kind="ExternalOutput").ap())
    gated_graph_network(nc, *args)
    result = run_bass_kernel_spmd(nc, [arrays], core_ids=[0])
    return result.results[0]["out_0"]
```

```python
import numpy as np
import concourse.bass as bass
from concourse import mybir

F32 = mybir.dt.float32
F32R = mybir.dt.float32r
I32 = mybir.dt.int32
ALU = mybir.AluOpType
ACT = mybir.ActivationFunctionType
AXIS = mybir.AxisListType

P = 128
BANK = 512
STEPS = 5
EPS = 1e-5


def gated_graph_network(nc, x, adj, in_W, in_b, out_W, out_b, r_W, r_b, z_W, z_b, h_W, h_b,
                        o1_W, o1_b, o2_W, o2_b, out):
    N, D = x.shape
    HALVES = D // P
    TILES = -(-N // P)
    ROWS = [min(P, N - j * P) for j in range(TILES)]
    CHUNKS = [(c, min(BANK, N - c)) for c in range(0, N, BANK)]
    NC = len(CHUNKS)
    TPC = BANK // P
    GATES = 3 * HALVES
    GW = 3 * D
    KT = 3 * HALVES
    FULL, LAST = TILES - 1, ROWS[-1]
    assert D == 2 * P and NC == 3 and TILES == 11 and FULL == 10

    STREAMED = [5, 6, 7, 8, 9]
    RESIDENT = [j for j in range(TILES) if j not in STREAMED]
    NS, NR = len(STREAMED), len(RESIDENT)

    base = -(-nc.sbuf_base // 32) * 32

    def place(name, shape, dt, at):
        size = int(np.prod(shape[1:])) * 4
        return nc.alloc_sbuf_tensor_at(name, shape, dt, offset=base + at), at + -(-size // 32) * 32

    at = 0
    an_at = at
    an_res, at = place("an_res", [P, NR, N], F32R, at)
    at_res, at = place("at_res", [P, NR, N], F32R, at)
    s_hi, at = place("s_hi", [P, TILES, D], F32R, at)
    slo_at = at
    s_lo, at = place("s_lo", [P, TILES, D], F32R, at)
    w_at = at
    w_hi, at = place("w_hi", [P, KT, GW], F32R, at)
    w_lo, at = place("w_lo", [P, KT, GW], F32R, at)
    degr_at = at
    deg_r, at = place("deg_r", [P, N], F32R, at)
    degc_at = at
    deg_c, at = place("deg_c", [P, N], F32R, at)
    st, at = place("st", [P, HALVES, N], F32, at)
    ring_at = at
    ring_n, at = place("ring_n", [P, NS, BANK], F32R, at)
    ring_t, at = place("ring_t", [P, NS, BANK], F32R, at)
    bias, at = place("bias", [P, GATES + HALVES], F32, at)
    image, at = place("image", [P, GATES, 2], F32, at)
    ident_r, at = place("ident_r", [P, P], F32R, at)
    ident = ident_r[:].bitcast(F32)
    row_sums, at = place("row_sums", [P, TILES], F32, at)
    o1_hi, at = place("o1_hi", [P, HALVES, D], F32R, at)
    o1_lo, at = place("o1_lo", [P, HALVES, D], F32R, at)
    work_at = at
    a_hi, at = place("a_hi", [P, 4, BANK], F32R, at)
    a_lo, at = place("a_lo", [P, 4, BANK], F32R, at)
    r_buf, at = place("r_buf", [P, HALVES, BANK], F32, at)
    z_buf, at = place("z_buf", [P, HALVES, BANK], F32, at)
    rs_hi, at = place("rs_hi", [P, HALVES, BANK], F32R, at)
    rs_lo, at = place("rs_lo", [P, HALVES, BANK], F32R, at)
    sc_at = at
    sc_hi, at = place("sc_hi", [P, HALVES, BANK], F32R, at)
    sc_lo, at = place("sc_lo", [P, HALVES, BANK], F32R, at)

    def hi_slot(kt):
        return (kt + HALVES) % KT

    w_nat, q = place("w_nat", [P, 3, HALVES, GW], F32, w_at + 4 * HALVES * GW)
    assert q <= w_at + 4 * GW * (KT + 2 * HALVES)
    x_nat, q = place("x_nat", [P, TILES, D], F32, slo_at)
    wt_f, q = place("wt_f", [P, 2 * HALVES, GW], F32, ring_at)
    io_nat, q = place("io_nat", [P, 2, HALVES, D], F32, q)
    o1_nat, q = place("o1_nat", [P, HALVES, D], F32, q)
    b_rows, q = place("b_rows", [P, 2, D], F32, q)
    assert q <= ring_at + 8 * NS * BANK
    tile_sum, _ = place("tile_sum", [P, N], F32R, degc_at)
    ident_raw, _ = place("ident_raw", [P, P], F32, degr_at)
    products, _ = place("products", [P, 2, 2 * HALVES, D], F32, sc_at)
    far_int, _ = place("far_int", [P, NS, N], I32, work_at)
    an_stage, q = place("an_stage", [P, NS, N], F32R, work_at)
    near_int, _ = place("near_int", [P, NR, N], I32, an_at)
    at_stage, q = place("at_stage", [P, 2, NS, P], F32R, q)
    ones_r, q = place("ones_r", [P, P], F32R, q)
    assert q <= sc_at
    x_end, q = place("x_end", [P, TILES, D], F32, an_at)
    o2_nat, q = place("o2_nat", [P, HALVES, D], F32, q)
    o_bias, q = place("o_bias", [P, D], F32, q)
    o2_hi, q = place("o2_hi", [P, HALVES, D], F32R, q)
    o2_lo, q = place("o2_lo", [P, HALVES, D], F32R, q)
    stats, q = place("stats", [P, TILES, 6], F32, q)
    mean_var, q = place("mean_var", [P, TILES, 2], F32, q)
    std, q = place("std", [P, TILES], F32, q)
    rstd, q = place("rstd", [P, TILES], F32, q)
    shift, q = place("shift", [P, TILES], F32, q)
    eps_col, q = place("eps_col", [P, 1], F32, q)
    assert q <= ring_at

    ps = nc.alloc_psum_tensor("ps", [P, 8, BANK], F32)
    ACC, GB, TB = 0, 4, 7

    far_n = nc.dram_tensor("far_n", [NS, P, N], F32, kind="Internal").ap()
    far_t = nc.dram_tensor("far_t", [NS, P, N], F32, kind="Internal").ap()

    S = nc.alloc_semaphore
    weights_in = [S(f"weights_in{g}") for g in range(3)]
    proj_in = S("proj_in")
    o1_in = S("o1_in")
    x_in = S("x_in")
    small_in = S("small_in")
    bias_in = S("bias_in")
    adj_in = [S(f"adj_in{i}") for i in range(TILES)]
    consts = S("consts")
    ones_ready = S("ones_ready")
    zeroed = S("zeroed")
    ident_r_ready = S("ident_r_ready")
    prep_ready = S("prep_ready")
    prep_act = S("prep_act")
    prep_dve = S("prep_dve")
    converted = S("converted")
    at_ready = S("at_ready")
    at_act = S("at_act")
    at_dve = S("at_dve")
    products_ready = S("products_ready")
    image_ready = S("image_ready")
    diag_ready = S("diag_ready")
    sums_done = S("sums_done")
    tiles_added = S("tiles_added")
    degrees_ready = S("degrees_ready")
    far_n_out = S("far_n_out")
    far_t_out = [S(f"far_t_out{b}") for b in range(2)]
    streamed_in = [S(f"streamed_in{k}") for k in range(NS)]
    streamed_used = [S(f"streamed_used{k}") for k in range(NS)]
    acc_ready = S("acc_ready")
    a_hi_ready = S("a_hi_ready")
    a_lo_ready = S("a_lo_ready")
    gate_ready = S("gate_ready")
    term_in = S("term_in")
    term_ready = S("term_ready")
    gate_sum = S("gate_sum")
    gate_act = S("gate_act")
    rs_ready = S("rs_ready")
    rs_hi_ready = S("rs_hi_ready")
    rs_lo_ready = S("rs_lo_ready")
    diff_ready = S("diff_ready")
    zdiff_ready = S("zdiff_ready")
    state_ready = S("state_ready")
    sc_hi_ready = S("sc_hi_ready")
    sc_lo_ready = S("sc_lo_ready")
    turned = S("turned")
    s_hi_ready = S("s_hi_ready")
    s_lo_ready = S("s_lo_ready")
    end_in = S("end_in")
    o_ready = S("o_ready")
    o_hi_ready = S("o_hi_ready")
    o_lo_ready = S("o_lo_ready")
    t_sum = S("t_sum")
    t_act = S("t_act")
    t_hi_ready = S("t_hi_ready")
    t_lo_ready = S("t_lo_ready")
    y_sum = S("y_sum")
    x_bias = S("x_bias")
    eps_ready = S("eps_ready")
    y_ready = S("y_ready")
    st_ready = S("st_ready")
    mv_ready = S("mv_ready")
    std_ready = S("std_ready")
    shift_ready = S("shift_ready")
    normed_act = S("normed_act")
    rstd_ready = S("rstd_ready")
    normed = S("normed")
    stored = S("stored")

    def tiles_of(c):
        return range(c * TPC, min((c + 1) * TPC, TILES))

    TURNS = [(8, 9), (10,), (0, 1), (2, 3), (4, 5), (6, 7)]
    NT = len(TURNS)
    NAT0, ST0, LO0 = NC + 1, HALVES * NC, 1

    POOL_TILES = 10
    GH = GW // 2
    WT = [("wt", k, b) for b in range(2) for k in range(2 * HALVES)]
    WS = [("ws", k, b) for b in range(2) for k in range(HALVES)]
    FOLD = [("fold", k, b) for k in range(2 * HALVES) for b in range(2)]
    ROW_SUMS = [("rows", c, 0) for c in range(NC - 1)]
    XT = [("xt", half * NC + c, 0) for c in range(NC) for half in range(HALVES)]
    A = [("A", i, 0) for i in range(TILES)]
    O1 = [("o1", 0, 0)]
    C = [("C", i, 0) for i in range(TILES)]
    SPLIT_HI = [("x_hi", c, 0) for c in range(NC)]
    SPLIT_LO = [("x_lo", c, 0) for c in range(NC)]
    FIRST_CHUNK = [("first_chunk", 0, 0)]
    DIAGONALS = [("diagonals", c, 0) for c in range(NC)]
    IMAGE = [("image", g, 0) for g in range(3)]
    PLAN = (C[0:1] + A[0:1] + WT[0:1] + WS[0:1] + WT[1:6] + WS[1:2] + WT[6:7] + C[1:2] + WT[7:8] + IMAGE[0:1]
            + WS[2:4] + IMAGE[1:2] + FOLD[0:1] + A[1:2] + IMAGE[2:3] + SPLIT_HI[0:1] + XT[0:1] + FOLD[1:2] + C[2:3]
            + FOLD[2:3] + XT[1:2] + C[3:4] + A[2:3] + XT[2:4] + FOLD[3:4] + C[4:5] + FOLD[4:5] + A[3:4]
            + SPLIT_HI[1:2] + XT[4:5] + DIAGONALS[0:1] + XT[5:6] + A[4:5] + C[5:7] + A[5:6] + SPLIT_LO[0:1]
            + ROW_SUMS[0:1] + A[6:7] + C[7:8] + SPLIT_LO[1:2] + FOLD[5:6] + C[8:9] + FOLD[6:7] + A[7:8]
            + SPLIT_HI[2:3] + A[8:9] + C[9:10] + O1 + DIAGONALS[1:2] + C[10:11] + A[9:10] + ROW_SUMS[1:2]
            + DIAGONALS[2:3] + FOLD[7:8] + A[10:11] + SPLIT_LO[2:3] + FIRST_CHUNK)
    PREP = [item for item in PLAN if item[0] in ("wt", "ws", "fold", "xt", "o1", "rows")]
    PREP_BANKS, AT_BANKS = (0, 1, 4, 5, 6), (2, 3, 7)
    SUM_BANK = GB

    def prep_dst(n, w=GH):
        return ps[:, PREP_BANKS[n % len(PREP_BANKS)], 0:w]

    def on_act(item):
        return item[0] in ("ws", "fold", "o1") or (item[0] == "wt" and item[1] % 2 == 0)

    def on_dve(item):
        return item[0] in ("ws", "fold", "rows", "o1") or (item[0] == "wt" and item[1] % 2 == 1)

    def prep_counts(n):
        done = PREP[:n + 1]
        return sum(map(on_act, done)), sum(map(on_dve, done)), sum(1 for k, _, _ in done if k == "xt")

    def wait_prep(eng, n):
        n_act, n_dve, n_xt = prep_counts(n)
        if n_act:
            eng.wait_ge(prep_act, n_act)
        if n_dve:
            eng.wait_ge(prep_dve, n_dve)
        if n_xt:
            eng.wait_ge(state_ready, n_xt)

    AT_GROUPS = [RESIDENT[0:4], [RESIDENT[4], RESIDENT[5], STREAMED[4]], STREAMED[0:4]]

    def an_tile(i):
        return an_res[:, RESIDENT.index(i), :] if i in RESIDENT else an_stage[:, STREAMED.index(i), :]

    def int_tile(i):
        return near_int[:, RESIDENT.index(i), :] if i in RESIDENT else far_int[:, STREAMED.index(i), :]

    def end_state(c, kt):
        cw = CHUNKS[c][1]
        if c % 2 == 0:
            return sc_hi[:, kt, 0:cw], sc_lo[:, kt, 0:cw]
        return a_hi[:, 2 + kt, 0:cw], a_lo[:, 2 + kt, 0:cw]

    def end_hidden(c, kt):
        cw = CHUNKS[c][1]
        if c % 2 == 0:
            return rs_hi[:, kt, 0:cw], rs_lo[:, kt, 0:cw]
        return a_hi[:, kt, 0:cw], a_lo[:, kt, 0:cw]

    def gate_buf(o):
        return (r_buf, z_buf, r_buf)[o // HALVES]

    def normed_by_act(j):
        return j < TPC or j % 2 == 1

    def state_cols(half, c):
        c0, cw = CHUNKS[c]
        return st[:, half, c0:c0 + cw]

    def nat_parts(c):
        ts = tiles_of(c)
        full = [t for t in ts if t < FULL]
        return [(P, full[0], full[-1] + 1)] + ([(LAST, FULL, TILES)] if ts[-1] == FULL else [])

    def w_slot(item):
        kind, k, b = item
        kt = 2 * HALVES + k if kind == "ws" else k
        return w_hi[:, hi_slot(kt), b * GH:(b + 1) * GH], w_lo[:, kt, b * GH:(b + 1) * GH]

    block = nc.Block()
    block.__enter__()

    @block.sync
    def _(sp):
        def load_adj(i):
            sp.dma_start(int_tile(i)[0:ROWS[i]], adj[i * P:i * P + ROWS[i], :]).then_inc(adj_in[i], 16)

        def store_rows(k):
            sp.wait_ge(converted, STREAMED[k] + 1)
            sp.dma_start(far_n[k], an_stage[:, k, :].bitcast(F32)).then_inc(far_n_out, 16)

        def store_blocks(i):
            sp.wait_ge(at_dve, 2 * (i + 1))
            sp.dma_start(far_t[:, :, i * P:i * P + ROWS[i]].rearrange("k p n -> p k n"),
                         at_stage[:, i % 2, :, 0:ROWS[i]].bitcast(F32)).then_inc(far_t_out[i % 2], 16)

        load_adj(0)
        for n, b in enumerate((in_b, out_b)):
            sp.dma_start(b_rows[:, n], b.rearrange("(a d) -> a d", a=1).to_broadcast([P, D])).then_inc(small_in, 16)
        for g, w in enumerate((r_W, z_W, h_W)):
            sp.dma_start(w_nat[:, g], w.rearrange("(m p) k -> p m k", p=P)).then_inc(weights_in[g], 16)
        for g, w in enumerate((in_W, out_W)):
            sp.dma_start(io_nat[:, g], w.rearrange("(m p) k -> p m k", p=P)).then_inc(proj_in, 16)
        load_adj(1)
        sp.dma_start(x_nat[:, 0:FULL], x[0:FULL * P, :].rearrange("(t p) d -> p t d", p=P)).then_inc(x_in, 16)
        sp.dma_start(x_nat[0:LAST, FULL], x[FULL * P:N, :]).then_inc(x_in, 16)
        load_adj(2)
        store_blocks(0)
        load_adj(3)
        store_blocks(1)
        load_adj(4)
        load_adj(5)
        store_blocks(2)
        load_adj(6)
        load_adj(7)
        store_blocks(3)
        load_adj(8)
        load_adj(9)
        store_blocks(4)
        store_blocks(5)
        load_adj(10)
        sp.dma_start(o1_nat[:], o1_W.rearrange("(m p) k -> p m k", p=P)).then_inc(o1_in, 16)
        store_rows(0)
        store_blocks(6)
        store_rows(1)
        store_blocks(7)
        store_rows(2)
        store_blocks(8)
        store_rows(3)
        sp.wait_ge(prep_ready, len(PREP))
        sp.wait_ge(far_t_out[0], 16 * 2)
        sp.wait_ge(far_t_out[1], 16 * 2)
        cw0 = CHUNKS[0][1]
        for k in range(NS):
            sp.wait_ge(converted, STREAMED[k] + 1)
            sp.dma_start(ring_n[:, k, 0:cw0].bitcast(F32),
                         an_stage[:, k, 0:cw0].bitcast(F32)).then_inc(streamed_in[k], 16)
            sp.dma_start(ring_t[:, k, 0:cw0].bitcast(F32), far_t[k, :, 0:cw0]).then_inc(streamed_in[k], 16)
        store_blocks(9)
        store_blocks(10)
        store_rows(4)
        sp.wait_ge(far_n_out, 16 * NS)
        sp.wait_ge(far_t_out[0], 16 * ((TILES + 1) // 2))
        sp.wait_ge(far_t_out[1], 16 * (TILES // 2))

        def stream(c, used):
            c0, cw = CHUNKS[c]
            for k in range(NS):
                sp.wait_ge(streamed_used[k], used)
                sp.dma_start(ring_n[:, k, 0:cw].bitcast(F32), far_n[k, :, c0:c0 + cw]).then_inc(streamed_in[k], 16)
                sp.dma_start(ring_t[:, k, 0:cw].bitcast(F32), far_t[k, :, c0:c0 + cw]).then_inc(streamed_in[k], 16)

        with sp.Fori(0, STEPS - 1) as i:
            for c in range(NC):
                stream((c + 1) % NC, i * NC + c + 1)
        for c in range(NC - 1):
            stream(c + 1, (STEPS - 1) * NC + c + 1)
        sp.wait_ge(acc_ready, 4 * NC * STEPS)
        sp.dma_start(o2_nat[:], o2_W.rearrange("(m p) k -> p m k", p=P)).then_inc(end_in, 16)
        sp.dma_start(o_bias[:, :], o2_b.rearrange("(a d) -> a d", a=1).to_broadcast([P, D])).then_inc(end_in, 16)
        sp.dma_start(x_end[:, 0:FULL], x[0:FULL * P, :].rearrange("(t p) d -> p t d", p=P)).then_inc(end_in, 16)
        sp.dma_start(x_end[0:LAST, FULL], x[FULL * P:N, :]).then_inc(end_in, 16)
        for c in range(NC):
            ts = tiles_of(c)
            n_act = sum(map(normed_by_act, range(ts[-1] + 1)))
            sp.wait_ge(normed_act, n_act)
            if n_act < ts[-1] + 1:
                sp.wait_ge(normed, ts[-1] + 1 - n_act)
            full = [t for t in ts if t < FULL]
            sp.dma_start(out[full[0] * P:(full[-1] + 1) * P, :].rearrange("(t p) d -> p t d", p=P),
                         x_end[:, full[0]:full[-1] + 1]).then_inc(stored, 16)
        sp.dma_start(out[FULL * P:N, :], x_end[0:LAST, FULL]).then_inc(stored, 16)
        sp.wait_ge(stored, 16 * (NC + 1))

    @block.gpsimd
    def _(pool):
        nc.gpsimd.memset(ident_raw[:], 0.0).then_inc(consts, 1)
        pool.wait_ge(consts, 1)
        nc.gpsimd.affine_select(out=ident_raw[:], in_=ident_raw[:], compare_op=ALU.not_equal, fill=1.0, base=0,
                                pattern=[[-1, P]], channel_multiplier=1).then_inc(consts, 1)
        for n, b in enumerate((r_b, z_b, h_b, o1_b)):
            pool.dma_start(bias[:, n * HALVES:(n + 1) * HALVES], b.rearrange("(m p) -> p m", p=P),
                           allow_slow_non_contiguous=True).then_inc(bias_in, 16)
        pool.wait_ge(small_in, 16 * 2)
        for g in range(3):
            pool.wait_ge(weights_in[g], 16)
            if g == 2:
                pool.wait_ge(image_ready, 1)
            nc.gpsimd.tensor_tensor(products[:, g % 2].rearrange("p (m w) d -> p m (w d)", m=HALVES),
                                    w_nat[:, g, :, 0:2 * D],
                                    b_rows[:].rearrange("p w d -> p (w d)").unsqueeze(1)
                                    .to_broadcast([P, HALVES, 2 * D]), ALU.mult).then_inc(products_ready, 1)
        for i in range(1, POOL_TILES):
            pool.wait_ge(converted, i + 1)
            first = an_tile(0)
            if i > 1:
                pool.wait_ge(tiles_added, i - 1)
                first = tile_sum[:]
            nc.gpsimd.tensor_tensor(tile_sum[:], first, an_tile(i), ALU.add).then_inc(tiles_added, 1)
        pool.wait_ge(end_in, 16 * 4)
        nc.gpsimd.tensor_tensor(x_end[:, 0:FULL], x_end[:, 0:FULL],
                                o_bias[:].unsqueeze(1).to_broadcast([P, FULL, D]), ALU.add).then_inc(x_bias, 1)
        nc.gpsimd.tensor_tensor(x_end[0:LAST, FULL], x_end[0:LAST, FULL], o_bias[0:LAST], ALU.add).then_inc(x_bias, 1)

    @block.tensor
    def _(pe):
        def three(dst, kt, cols, hi, lo, start, stop, wh=w_hi, wl=w_lo):
            ks = hi_slot(kt) if wh is w_hi else kt
            nc.tensor.matmul(dst, wh[:, ks, cols], hi, start=start, stop=False)
            nc.tensor.matmul(dst, wh[:, ks, cols], lo, start=False, stop=False)
            return nc.tensor.matmul(dst, wl[:, kt, cols], hi, start=False, stop=stop)

        def weight_bank(n, item):
            kind, k, b = item
            if n >= len(PREP_BANKS):
                wait_prep(pe, n - len(PREP_BANKS))
            dst = prep_dst(n)
            if kind in ("wt", "ws"):
                qt = k if kind == "wt" else 2 * HALVES + k
                for o in range(3 * b, 3 * b + 3):
                    g, m = divmod(o, HALVES)
                    if kind == "wt" and k == 0:
                        pe.wait_ge(weights_in[g], 16)
                    last = nc.tensor.transpose(dst[:, (o % 3) * P:(o % 3 + 1) * P],
                                               w_nat[:, g, m, qt * P:(qt + 1) * P], ident)
            elif kind == "fold":
                which, kt = divmod(k, HALVES)
                for qh in range(HALVES):
                    last = nc.tensor.matmul(dst, io_nat[:, which, qh, kt * P:(kt + 1) * P],
                                            wt_f[:, which * HALVES + qh, b * GH:(b + 1) * GH],
                                            start=(qh == 0), stop=(qh == HALVES - 1))
            elif kind == "rows":
                pe.wait_ge(diag_ready, k + 1)
                c0, cw = CHUNKS[k]
                last = nc.tensor.matmul(prep_dst(n, cw), ones_r[:], deg_r[:, c0:c0 + cw], start=True, stop=True)
            elif kind == "xt":
                half, c = divmod(k, NC)
                for j in tiles_of(c):
                    r = ROWS[j]
                    last = nc.tensor.transpose(prep_dst(n, BANK)[:, (j % TPC) * P:(j % TPC) * P + r],
                                               x_nat[0:r, j, half * P:(half + 1) * P], ident[0:r, 0:r])
            else:
                for kt in range(HALVES):
                    for m in range(HALVES):
                        last = nc.tensor.transpose(prep_dst(n, BANK)[:, kt * D + m * P:kt * D + (m + 1) * P],
                                                   o1_nat[:, m, kt * P:(kt + 1) * P], ident)
            last.then_inc(prep_ready, 1)

        def adjacency_tile(i):
            r, tile = ROWS[i], an_tile(i)
            pe.wait_ge(converted, i + 1)
            for g, group in enumerate(AT_GROUPS):
                if i > 0:
                    if g == 0:
                        pe.wait_ge(at_act, i)
                    else:
                        pe.wait_ge(at_dve, 2 * (i - 1) + g)
                for k, j in enumerate(group):
                    last = nc.tensor.matmul(ps[0:ROWS[j], AT_BANKS[g], k * P:k * P + r],
                                            tile[0:r, j * P:j * P + ROWS[j]], ident_r[0:r, 0:r],
                                            start=True, stop=True)
                last.then_inc(at_ready, 1)

        def degree_sums():
            for rows in (an_tile(TILES - 1)[0:LAST], tile_sum[:]):
                if rows.shape[0] == P:
                    pe.wait_ge(tiles_added, POOL_TILES - 1)
                for c, (c0, cw) in enumerate(CHUNKS):
                    last = nc.tensor.matmul(ps[:, SUM_BANK + c, 0:cw], ones_r[0:rows.shape[0]],
                                            rows[:, c0:c0 + cw], start=rows.shape[0] < P, stop=rows.shape[0] == P,
                                            skip_group_check=True)
            last.then_inc(sums_done, 1)
            pe.wait_ge(at_dve, 2 * TILES)
            pe.wait_ge(diag_ready, NC)
            nc.tensor.matmul(ps[:, AT_BANKS[2], 0:cw], ones_r[:], deg_r[:, c0:c0 + cw],
                             start=True, stop=True).then_inc(sums_done, 1)

        pe.wait_ge(ident_r_ready, 1)
        arrivals = {"fold": (proj_in, 16 * 2), "xt": (x_in, 16 * 2), "o1": (o1_in, 16)}
        n = 0
        for item in PLAN:
            kind, k, b = item
            if kind in arrivals and k == 0 and b == 0:
                pe.wait_ge(*arrivals[kind])
            if item == ROW_SUMS[0]:
                pe.wait_ge(ones_ready, 1)
            if kind == "A":
                adjacency_tile(k)
            elif item in PREP:
                weight_bank(n, item)
                n += 1
        wait_prep(pe, len(PREP) - 1)
        degree_sums()
        pe.wait_ge(at_act, TILES)

        def turn(i, t):
            pe.wait_ge(s_lo_ready, NAT0 + i * NT + t)
            for n, j in enumerate(TURNS[t]):
                for half in range(HALVES):
                    last = nc.tensor.transpose(ps[0:ROWS[j], TB, n * D + half * P:n * D + (half + 1) * P],
                                               st[:, half, j * P:j * P + ROWS[j]], ident)
            last.then_inc(turned, 1)

        def aggregate(i, c):
            c0, cw = CHUNKS[c]
            pe.wait_ge(a_lo_ready, LO0 + i * 4 * NC + 4 * c)
            if c == 0:
                pe.wait_ge(s_hi_ready, NAT0 + i * NT)
                pe.wait_ge(s_lo_ready, NAT0 + i * NT)
            for j in range(TILES):
                r = ROWS[j]
                if c == 0 and j == 6:
                    pe.wait_ge(degrees_ready, 1)
                    pe.wait_ge(state_ready, ST0 + i * NC * HALVES)
                    turn(i, 0)
                if c == 0 and j == 7:
                    turn(i, 1)
                if c == 0 and j == TURNS[0][0]:
                    pe.wait_ge(s_hi_ready, NAT0 + i * NT + 1)
                    pe.wait_ge(s_lo_ready, NAT0 + i * NT + 1)
                if c == 0 and j == TURNS[1][0]:
                    pe.wait_ge(s_hi_ready, NAT0 + i * NT + 2)
                    pe.wait_ge(s_lo_ready, NAT0 + i * NT + 2)
                if j in STREAMED:
                    k = STREAMED.index(j)
                    pe.wait_ge(streamed_in[k], i * 32 * NC + 32 * (c + 1))
                    rows_t, rows_n = ring_t[0:r, k, 0:cw], ring_n[0:r, k, 0:cw]
                else:
                    k = RESIDENT.index(j)
                    rows_t, rows_n = at_res[0:r, k, c0:c0 + cw], an_res[0:r, k, c0:c0 + cw]
                for q in range(4):
                    rows, half = (rows_t, rows_n)[q // HALVES], q % HALVES
                    dst = ps[:, ACC + q, 0:cw]
                    nc.tensor.matmul(dst, s_hi[0:r, j, half * P:(half + 1) * P], rows, start=(j == 0), stop=False)
                    last = nc.tensor.matmul(dst, s_lo[0:r, j, half * P:(half + 1) * P], rows, start=False,
                                            stop=(j == TILES - 1))
                    if j == TILES - 1:
                        last.then_inc(acc_ready, 1)
                if j in STREAMED:
                    last.then_inc(streamed_used[STREAMED.index(j)], 1)

        def gates(i, c):
            c0, cw = CHUNKS[c]
            g0 = i * GATES * NC + GATES * c
            base4 = i * 4 * NC + 4 * c
            base2 = i * HALVES * NC + HALVES * c

            def dst(o):
                return ps[:, GB + o % 3, 0:cw]

            def state_part(o):
                for half in range(HALVES):
                    three(dst(o), 2 * HALVES + half, slice(o * P, (o + 1) * P),
                          sc_hi[:, half, 0:cw], sc_lo[:, half, 0:cw], half == 0, False)

            def sums_part(o, start, stop):
                for q in range(4):
                    if o == 0:
                        pe.wait_ge(a_hi_ready, base4 + q + 1)
                        pe.wait_ge(a_lo_ready, LO0 + base4 + q + 1)
                    last = three(dst(o), q, slice(o * P, (o + 1) * P), a_hi[:, q, 0:cw], a_lo[:, q, 0:cw],
                                 start and q == 0, stop and q == 3)
                return last

            if c > 0:
                pe.wait_ge(gate_sum, g0)
            pe.wait_ge(sc_hi_ready, base2 + HALVES)
            pe.wait_ge(sc_lo_ready, base2 + HALVES)
            for o in range(3):
                state_part(o)
            if c == NC - 1:
                turn(i, 2)
            for o in range(4):
                if o == 3:
                    pe.wait_ge(gate_sum, g0 + 1)
                    state_part(o)
                sums_part(o, False, True).then_inc(gate_ready, 1)
                if c == NC - 1 and o > 0:
                    turn(i, 2 + o)
            for o in range(4, GATES):
                pe.wait_ge(gate_sum, g0 + o - 2)
                sums_part(o, True, False)
                for half in range(HALVES):
                    if o == 4:
                        pe.wait_ge(rs_hi_ready, base2 + half + 1)
                        pe.wait_ge(rs_lo_ready, base2 + half + 1)
                    last = three(dst(o), 2 * HALVES + half, slice(o * P, (o + 1) * P),
                                 rs_hi[:, half, 0:cw], rs_lo[:, half, 0:cw], False, half == HALVES - 1)
                last.then_inc(gate_ready, 1)

        with pe.Fori(0, STEPS) as i:
            for c in range(NC):
                aggregate(i, c)
                gates(i, c)

        def hidden(c):
            cw = CHUNKS[c][1]
            n_sc = HALVES * (NC * STEPS + c + 1)
            pe.wait_ge(sc_hi_ready, n_sc)
            pe.wait_ge(sc_lo_ready, n_sc)
            for m in range(HALVES):
                n = HALVES * c + m
                if n >= 3:
                    pe.wait_ge(t_act, n - 2)
                elif n > 0:
                    pe.wait_ge(gate_sum, GATES * NC * STEPS - 2 + n)
                dst = ps[:, GB + n % 3, 0:cw]
                for kt in range(HALVES):
                    hi, lo = end_state(c, kt)
                    last = three(dst, 0, slice(m * P, (m + 1) * P), hi, lo, kt == 0, kt == HALVES - 1,
                                 o1_hi[:, kt:kt + 1], o1_lo[:, kt:kt + 1])
                last.then_inc(t_sum, 1)

        def head(c):
            pe.wait_ge(t_hi_ready, HALVES * (c + 1))
            pe.wait_ge(t_lo_ready, HALVES * (c + 1))
            for j in tiles_of(c):
                r = ROWS[j]
                if j >= 4:
                    pe.wait_ge(y_ready, j - 3)
                dst = ps[0:r, ACC + j % 4, 0:D]
                off = (j % TPC) * P
                for kt in range(HALVES):
                    hi, lo = end_hidden(c, kt)
                    hi, lo = hi[:, off:off + r], lo[:, off:off + r]
                    nc.tensor.matmul(dst, hi, o2_hi[:, kt], start=(kt == 0), stop=False)
                    nc.tensor.matmul(dst, hi, o2_lo[:, kt], start=False, stop=False)
                    last = nc.tensor.matmul(dst, lo, o2_hi[:, kt], start=False, stop=(kt == HALVES - 1))
                last.then_inc(y_sum, 1)

        pe.wait_ge(gate_sum, GATES * NC * STEPS - 2)
        hidden(0)
        pe.wait_ge(end_in, 16 * 4)
        for kt in range(HALVES):
            for m in range(HALVES):
                last = nc.tensor.transpose(ps[:, TB, kt * D + m * P:kt * D + (m + 1) * P],
                                           o2_nat[:, m, kt * P:(kt + 1) * P], ident)
        last.then_inc(o_ready, 1)
        hidden(1)
        pe.wait_ge(o_hi_ready, 1)
        pe.wait_ge(o_lo_ready, 1)
        head(0)
        hidden(2)
        head(1)
        head(2)

    @block.scalar
    def _(act):
        act.wait_ge(consts, 2)
        nc.scalar.copy(ident_r[:], ident_raw[:]).then_inc(ident_r_ready, 1)

        def convert(i):
            act.wait_ge(adj_in[i], 16)
            r = ROWS[i]
            nc.scalar.activation(an_tile(i)[0:r], int_tile(i)[0:r], ACT.Copy,
                                 accum_out=row_sums[0:r, i:i + 1]).then_inc(converted, 1)

        act.wait_ge(zeroed, 1)
        n = 0
        for item in PLAN:
            kind, k, b = item
            if kind == "C":
                convert(k)
                continue
            if kind == "x_hi":
                act.wait_ge(x_in, 16 * 2)
                for rows, a, e in nat_parts(k):
                    nc.scalar.copy(s_hi[0:rows, a:e], x_nat[0:rows, a:e]).then_inc(s_hi_ready, 1)
                continue
            if kind == "first_chunk":
                act.wait_ge(state_ready, HALVES)
                for half in range(HALVES):
                    nc.scalar.copy(sc_hi[:, half, 0:CHUNKS[0][1]], state_cols(half, 0)).then_inc(sc_hi_ready, 1)
                continue
            if item not in PREP and kind != "A":
                continue
            if kind == "A":
                act.wait_ge(at_ready, 3 * k + 1)
                r = ROWS[k]
                nc.scalar.copy(at_res[:, 0:4, k * P:k * P + r],
                               ps[:, AT_BANKS[0]].rearrange("p (k n) -> p k n", k=4)[:, :, 0:r]).then_inc(at_act, 1)
                continue
            if on_act(item):
                act.wait_ge(prep_ready, n + 1)
                if item == FOLD[0]:
                    act.wait_ge(products_ready, 3)
                if kind == "wt":
                    dst, src = wt_f[:, k, b * GH:(b + 1) * GH], prep_dst(n)
                elif kind == "o1":
                    dst, src = o1_hi[:].rearrange("p k n -> p (k n)"), prep_dst(n, BANK)
                else:
                    dst, src = w_slot(item)[0], prep_dst(n)
                nc.scalar.copy(dst, src).then_inc(prep_act, 1)
            n += 1

        act.wait_ge(far_n_out, 16 * NS)
        act.wait_ge(far_t_out[0], 16 * ((TILES + 1) // 2))
        act.wait_ge(far_t_out[1], 16 * (TILES // 2))
        act.wait_ge(bias_in, 16 * 4)

        def split_state(i, c, n):
            act.wait_ge(state_ready, n)
            for half in range(HALVES):
                nc.scalar.copy(sc_hi[:, half, 0:CHUNKS[c][1]], state_cols(half, c)).then_inc(sc_hi_ready, 1)

        def turned_hi(i, t):
            act.wait_ge(turned, i * NT + t + 1)
            js = TURNS[t]
            r = ROWS[js[0]]
            nc.scalar.copy(s_hi[0:r, js[0]:js[-1] + 1],
                           ps[0:r, TB, 0:D * len(js)].rearrange("p (t d) -> p t d", d=D)).then_inc(s_hi_ready, 1)

        with act.Fori(0, STEPS) as i:
            turned_hi(i, 0)
            turned_hi(i, 1)
            for c, (c0, cw) in enumerate(CHUNKS):
                base4 = i * 4 * NC + 4 * c
                g0 = i * GATES * NC + GATES * c
                base2 = i * HALVES * NC + HALVES * c
                for q in range(4):
                    act.wait_ge(acc_ready, base4 + q + 1)
                    nc.scalar.copy(a_hi[:, q, 0:cw], ps[:, ACC + q, 0:cw]).then_inc(a_hi_ready, 1)
                if c == NC - 1:
                    turned_hi(i, 2)
                for o in range(GATES):
                    g, half = divmod(o, HALVES)
                    buf = gate_buf(o)[:, half, 0:cw]
                    act.wait_ge(gate_sum, g0 + o + 1)
                    nc.scalar.activation(buf, buf, ACT.Tanh if g == 2 else ACT.Sigmoid,
                                         bias=bias[:, o:o + 1]).then_inc(gate_act, 1)
                    if c == NC - 1 and 0 < o < 4:
                        turned_hi(i, 2 + o)
                    if g == 0:
                        act.wait_ge(rs_ready, base2 + half + 1)
                        nc.scalar.copy(rs_hi[:, half, 0:cw], r_buf[:, half, 0:cw]).then_inc(rs_hi_ready, 1)
                    if o == 2 * HALVES - 1:
                        if c < NC - 1:
                            split_state(i, c + 1, ST0 + i * HALVES * NC)
                        else:
                            split_state(i, 0, ST0 + i * HALVES * NC + HALVES)

        def tanh(c):
            cw = CHUNKS[c][1]
            for m in range(HALVES):
                n = HALVES * c + m
                act.wait_ge(t_sum, n + 1)
                if c >= 1:
                    act.wait_ge(t_lo_ready, n - 1)
                if c == 0:
                    act.wait_ge(state_ready, ST0 + HALVES * NC * STEPS)
                nc.scalar.activation(z_buf[:, m, 0:cw], ps[:, GB + n % 3, 0:cw], ACT.Tanh,
                                     bias=bias[:, GATES + m:GATES + m + 1]).then_inc(t_act, 1)
                act.wait_ge(t_act, n + 1)
                if c >= 2:
                    act.wait_ge(y_sum, tiles_of(c - 2)[-1] + 1)
                nc.scalar.copy(end_hidden(c, m)[0], z_buf[:, m, 0:cw]).then_inc(t_hi_ready, 1)

        def end_split(c):
            act.wait_ge(state_ready, ST0 + HALVES * (NC * STEPS - NC + c + 1))
            if c == 1:
                act.wait_ge(gate_ready, GATES * NC * STEPS)
            if c >= 2:
                act.wait_ge(t_sum, HALVES * (c - 1))
            for kt in range(HALVES):
                nc.scalar.copy(end_state(c, kt)[0], state_cols(kt, c)).then_inc(sc_hi_ready, 1)

        end_split(1)
        tanh(0)
        act.wait_ge(o_ready, 1)
        nc.scalar.copy(o2_hi[:].rearrange("p k n -> p (k n)"), ps[:, TB, :]).then_inc(o_hi_ready, 1)
        end_split(2)
        tanh(1)
        tanh(2)
        act.wait_ge(eps_ready, 1)

        def deviation(c):
            act.wait_ge(mv_ready, tiles_of(c)[-1] + 1)
            for r, a, b in nat_parts(c):
                nc.scalar.activation(std[0:r, a:b], mean_var[0:r, a:b, 1], ACT.Sqrt,
                                     bias=eps_col[0:r, 0:1]).then_inc(std_ready, 1)

        def normalise(c):
            act.wait_ge(shift_ready, c + len(nat_parts(c)))
            for j in tiles_of(c):
                if normed_by_act(j):
                    nc.scalar.activation(x_end[:, j], x_end[:, j], ACT.Identity, bias=shift[:, j:j + 1],
                                         scale=rstd[:, j:j + 1]).then_inc(normed_act, 1)

        deviation(0)
        normalise(0)
        deviation(1)
        deviation(2)
        normalise(1)
        normalise(2)

    @block.vector
    def _(dve):
        nc.vector.memset(row_sums[:], 0.0).then_inc(zeroed, 1)
        nc.vector.memset(ones_r[:].bitcast(F32), 1.0).then_inc(ones_ready, 1)
        n = 0
        for item in PLAN:
            kind, k, b = item
            if kind == "A":
                r = ROWS[k]
                if k >= 2:
                    dve.wait_ge(far_t_out[k % 2], 16 * (k // 2))
                dve.wait_ge(at_ready, 3 * k + 2)
                b1 = ps[:, AT_BANKS[1]]
                nc.vector.tensor_copy(at_res[:, 4, k * P:k * P + r], b1[:, 0:r])
                nc.vector.tensor_copy(at_res[0:LAST, 5, k * P:k * P + r], b1[0:LAST, P:P + r])
                nc.vector.tensor_copy(at_stage[:, k % 2, 4, 0:r], b1[:, 2 * P:2 * P + r]).then_inc(at_dve, 1)
                dve.wait_ge(at_ready, 3 * k + 3)
                nc.vector.tensor_copy(at_stage[:, k % 2, 0:4, 0:r],
                                      ps[:, AT_BANKS[2]].rearrange("p (k n) -> p k n", k=4)[:, :, 0:r]
                                      ).then_inc(at_dve, 1)
                continue
            if kind == "image":
                dve.wait_ge(products_ready, k + 1)
                nc.vector.tensor_reduce(image[:, k * HALVES:(k + 1) * HALVES].rearrange("p o w -> p (o w)"),
                                        products[:, k % 2], AXIS.X, ALU.add).then_inc(image_ready, 1)
                continue
            if kind == "diagonals":
                ts = tiles_of(k)
                full = min(ts[-1] + 1, FULL)
                dve.wait_ge(converted, ts[-1] + 1)
                dve.wait_ge(ident_r_ready, 1)
                op = nc.vector.tensor_tensor(
                    deg_r[:, ts[0] * P:full * P].rearrange("p (t n) -> p t n", n=P),
                    ident.unsqueeze(1).to_broadcast([P, full - ts[0], P]),
                    row_sums[:, ts[0]:full].unsqueeze(2).to_broadcast([P, full - ts[0], P]), ALU.mult)
                if ts[-1] == FULL:
                    op.then_inc(a_lo_ready, LO0)
                    op = nc.vector.tensor_scalar(deg_r[:, FULL * P:N], ident[:, 0:LAST], row_sums[:, FULL:TILES],
                                                 None, ALU.mult)
                op.then_inc(diag_ready, 1)
                continue
            if kind == "x_lo":
                dve.wait_ge(prep_ready, PREP.index(XT[HALVES * k + 1]) + 1)
                for p, (rows, a, e) in enumerate(nat_parts(k)):
                    dve.wait_ge(s_hi_ready, k + p + 1)
                    nc.vector.tensor_tensor(s_lo[0:rows, a:e], x_nat[0:rows, a:e], s_hi[0:rows, a:e].bitcast(F32),
                                            ALU.subtract).then_inc(s_lo_ready, 1)
                continue
            if kind == "first_chunk":
                dve.wait_ge(state_ready, HALVES)
                for half in range(HALVES):
                    cw = CHUNKS[0][1]
                    dve.wait_ge(sc_hi_ready, half + 1)
                    nc.vector.tensor_tensor(sc_lo[:, half, 0:cw], state_cols(half, 0),
                                            sc_hi[:, half, 0:cw].bitcast(F32), ALU.subtract).then_inc(sc_lo_ready, 1)
                continue
            if item not in PREP:
                continue
            if kind == "xt":
                half, c = divmod(k, NC)
                dve.wait_ge(prep_ready, n + 1)
                nc.vector.tensor_copy(state_cols(half, c), prep_dst(n, CHUNKS[c][1])).then_inc(state_ready, 1)
            elif on_dve(item):
                dve.wait_ge(prep_ready, n + 1)
                if kind == "wt":
                    nc.vector.tensor_copy(wt_f[:, k, b * GH:(b + 1) * GH], prep_dst(n)).then_inc(prep_dve, 1)
                else:
                    dve.wait_ge(prep_act, prep_counts(n)[0])
                    if kind == "rows":
                        c0, cw = CHUNKS[k]
                        nc.vector.tensor_copy(deg_r[:, c0:c0 + cw], prep_dst(n, cw)).then_inc(prep_dve, 1)
                    elif kind == "o1":
                        hi = o1_hi[:].rearrange("p k n -> p (k n)")
                        nc.vector.tensor_tensor(o1_lo[:].rearrange("p k n -> p (k n)"), prep_dst(n, BANK),
                                                hi.bitcast(F32), ALU.subtract).then_inc(prep_dve, 1)
                    else:
                        hi, lo = w_slot(item)
                        nc.vector.tensor_tensor(lo, prep_dst(n), hi.bitcast(F32), ALU.subtract).then_inc(prep_dve, 1)
            n += 1
        dve.wait_ge(sums_done, 1)
        for c, (c0, cw) in enumerate(CHUNKS):
            nc.vector.tensor_copy(deg_c[:, c0:c0 + cw], ps[:, SUM_BANK + c, 0:cw])
        dve.wait_ge(sums_done, 2)
        nc.vector.tensor_copy(deg_r[:, c0:c0 + cw], ps[:, AT_BANKS[2], 0:cw]).then_inc(degrees_ready, 1)
        dve.wait_ge(degrees_ready, 1)
        dve.wait_ge(image_ready, 3)

        def bias_terms(i, c, g):
            c0, cw = CHUNKS[c]
            n = i * GATES * NC + GATES * c + HALVES * g
            rows, cols = deg_r[:, c0:c0 + cw].bitcast(F32), deg_c[:, c0:c0 + cw].bitcast(F32)
            for half in range(HALVES):
                o = g * HALVES + half
                nc.vector.tensor_scalar(gate_buf(o)[:, half, 0:cw], rows, image[:, o, 0:1], None,
                                        ALU.mult).then_inc(term_in, 1)
            for half in range(HALVES):
                o = g * HALVES + half
                buf = gate_buf(o)[:, half, 0:cw]
                dve.wait_ge(term_in, n + half + 1)
                nc.vector.scalar_tensor_tensor(out=buf, in0=cols, scalar=image[:, o, 1:2], in1=buf,
                                               op0=ALU.mult, op1=ALU.add).then_inc(term_ready, 1)

        def add_sums(i, c, o):
            cw = CHUNKS[c][1]
            n = i * GATES * NC + GATES * c + o
            buf = gate_buf(o)[:, o % HALVES, 0:cw]
            dve.wait_ge(term_ready, n + 1)
            dve.wait_ge(gate_ready, n + 1)
            nc.vector.tensor_tensor(buf, ps[:, GB + o % 3, 0:cw], buf, ALU.add).then_inc(gate_sum, 1)

        def turned_lo(i, t):
            dve.wait_ge(s_hi_ready, NAT0 + i * NT + t + 1)
            js = TURNS[t]
            r = ROWS[js[0]]
            nc.vector.tensor_tensor(s_lo[0:r, js[0]:js[-1] + 1],
                                    ps[0:r, TB, 0:D * len(js)].rearrange("p (t d) -> p t d", d=D),
                                    s_hi[0:r, js[0]:js[-1] + 1].bitcast(F32),
                                    ALU.subtract).then_inc(s_lo_ready, 1)

        def split_lo(hi, lo, src, n):
            dve.wait_ge(sc_hi_ready, n)
            nc.vector.tensor_tensor(lo, src, hi.bitcast(F32), ALU.subtract).then_inc(sc_lo_ready, 1)

        with dve.Fori(0, STEPS) as i:
            turned_lo(i, 0)
            turned_lo(i, 1)
            for c, (c0, cw) in enumerate(CHUNKS):
                base4 = i * 4 * NC + 4 * c
                g0 = i * GATES * NC + GATES * c
                base2 = i * HALVES * NC + HALVES * c
                dve.wait_ge(state_ready, ST0 + base2)
                bias_terms(i, c, 0)
                bias_terms(i, c, 1)
                for q in range(4):
                    dve.wait_ge(a_hi_ready, base4 + q + 1)
                    nc.vector.tensor_tensor(a_lo[:, q, 0:cw], ps[:, ACC + q, 0:cw], a_hi[:, q, 0:cw].bitcast(F32),
                                            ALU.subtract).then_inc(a_lo_ready, 1)
                if c == NC - 1:
                    turned_lo(i, 2)
                for o in range(2 * HALVES):
                    add_sums(i, c, o)
                    if 1 <= o < HALVES + 1:
                        dve.wait_ge(rs_hi_ready, base2 + o)
                        nc.vector.tensor_tensor(rs_lo[:, o - 1, 0:cw], r_buf[:, o - 1, 0:cw],
                                                rs_hi[:, o - 1, 0:cw].bitcast(F32),
                                                ALU.subtract).then_inc(rs_lo_ready, 1)
                    if o < HALVES:
                        dve.wait_ge(gate_act, g0 + o + 1)
                        nc.vector.tensor_tensor(r_buf[:, o, 0:cw], r_buf[:, o, 0:cw], state_cols(o, c),
                                                ALU.mult).then_inc(rs_ready, 1)
                    if c == NC - 1 and o > 0:
                        turned_lo(i, 2 + o)
                dve.wait_ge(rs_lo_ready, base2 + HALVES)
                bias_terms(i, c, 2)
                nxt = (c + 1) % NC
                w = CHUNKS[nxt][1]
                for half in range(HALVES):
                    split_lo(sc_hi[:, half, 0:w], sc_lo[:, half, 0:w], state_cols(half, nxt),
                             base2 + HALVES + half + 1)
                for half in range(HALVES):
                    s, z, h = state_cols(half, c), z_buf[:, half, 0:cw], r_buf[:, half, 0:cw]
                    add_sums(i, c, 2 * HALVES + half)
                    dve.wait_ge(gate_act, g0 + 2 * HALVES + half + 1)
                    nc.vector.tensor_tensor(h, h, s, ALU.subtract).then_inc(diff_ready, 1)
                    dve.wait_ge(diff_ready, base2 + half + 1)
                    nc.vector.tensor_tensor(h, h, z, ALU.mult).then_inc(zdiff_ready, 1)
                    dve.wait_ge(zdiff_ready, base2 + half + 1)
                    nc.vector.tensor_tensor(s, s, h, ALU.add).then_inc(state_ready, 1)

        dve.wait_ge(end_in, 16 * 4)
        nc.vector.memset(eps_col[:], EPS).then_inc(eps_ready, 1)

        def o2_low():
            dve.wait_ge(o_hi_ready, 1)
            nc.vector.tensor_tensor(o2_lo[:].rearrange("p k n -> p (k n)"), ps[:, TB, :],
                                    o2_hi[:].rearrange("p k n -> p (k n)").bitcast(F32),
                                    ALU.subtract).then_inc(o_lo_ready, 1)

        def end_split_lo(c):
            for kt in range(HALVES):
                hi, lo = end_state(c, kt)
                split_lo(hi, lo, state_cols(kt, c), HALVES * (NC * STEPS + c) + kt + 1)

        def hidden_lo(c):
            for m in range(HALVES):
                hi, lo = end_hidden(c, m)
                dve.wait_ge(t_hi_ready, HALVES * c + m + 1)
                nc.vector.tensor_tensor(lo, z_buf[:, m, 0:CHUNKS[c][1]], hi.bitcast(F32),
                                        ALU.subtract).then_inc(t_lo_ready, 1)

        def rows_out(js):
            for n in range(len(js) + 2):
                if n < len(js):
                    j = js[n]
                    y = x_end[0:ROWS[j], j]
                    dve.wait_ge(y_sum, j + 1)
                    nc.vector.tensor_tensor(y, ps[0:ROWS[j], ACC + j % 4, 0:D], y, ALU.add).then_inc(y_ready, 1)
                if 1 <= n < len(js) + 1:
                    j = js[n - 1]
                    dve.wait_ge(y_ready, j + 1)
                    nc.vector.bn_stats(stats[0:ROWS[j], j], x_end[0:ROWS[j], j]).then_inc(st_ready, 1)
                if n >= 2:
                    j = js[n - 2]
                    dve.wait_ge(st_ready, j + 1)
                    nc.vector.bn_aggr(mean_var[0:ROWS[j], j], stats[0:ROWS[j], j]).then_inc(mv_ready, 1)

        def normalise(c):
            ts = tiles_of(c)
            parts = nat_parts(c)
            for n, (r, a, b) in enumerate(parts):
                dve.wait_ge(std_ready, c + n + 1)
                nc.vector.reciprocal(rstd[0:r, a:b], std[0:r, a:b]).then_inc(rstd_ready, 1)
            for n, (r, a, b) in enumerate(parts):
                dve.wait_ge(rstd_ready, c + n + 1)
                nc.vector.scalar_tensor_tensor(out=shift[0:r, a:b], in0=mean_var[0:r, a:b, 0], scalar=-1.0,
                                               in1=rstd[0:r, a:b], op0=ALU.mult, op1=ALU.mult).then_inc(shift_ready, 1)
            for j in ts:
                if not normed_by_act(j):
                    r = ROWS[j]
                    nc.vector.tensor_scalar(x_end[0:r, j], x_end[0:r, j], mean_var[0:r, j, 0:1], rstd[0:r, j:j + 1],
                                            ALU.subtract, ALU.mult).then_inc(normed, 1)

        end_split_lo(1)
        hidden_lo(0)
        o2_low()
        end_split_lo(2)
        hidden_lo(1)
        dve.wait_ge(x_bias, 2)
        rows_out(tiles_of(0))
        hidden_lo(2)
        rows_out(tiles_of(1))
        normalise(0)
        rows_out(tiles_of(2))
        normalise(1)
        normalise(2)

    block.__exit__(None, None, None)


_INS = ["x", "adj", "L0_gnn_in_W", "L0_gnn_in_b", "L0_gnn_out_W", "L0_gnn_out_b", "L0_gnn_r_W", "L0_gnn_r_b",
        "L0_gnn_z_W", "L0_gnn_z_b", "L0_gnn_h_W", "L0_gnn_h_b", "L0_gnn_o1_W", "L0_gnn_o1_b", "L0_gnn_o2_W",
        "L0_gnn_o2_b"]


def kernel(**inputs):
    import concourse.bacc as bacc
    from concourse.bass_utils import run_bass_kernel_spmd

    nc = bacc.Bacc("TRN2", target_bir_lowering=False, num_devices=1)
    arrays, args = {}, []
    for name in _INS:
        a = np.ascontiguousarray(inputs[name])
        arrays[f"in_{name}"] = a
        args.append(nc.dram_tensor(f"in_{name}", a.shape, mybir.dt.from_np(a.dtype), kind="ExternalInput").ap())
    shape = inputs["x"].shape
    args.append(nc.dram_tensor("out_0", shape, F32, kind="ExternalOutput").ap())
    gated_graph_network(nc, *args)
    result = run_bass_kernel_spmd(nc, [arrays], core_ids=[0])
    return result.results[0]["out_0"]
```
